# Optimizing a Trainium2 kernel written in Bass

```python
import numpy as np
import jax
import jax.numpy as jnp

def _softmax(x, axis=-1):
    return jax.nn.softmax(x, axis=axis)

def _gelu(x):
    return jax.nn.gelu(x, approximate=True)

def _silu(x):
    return jax.nn.silu(x)

def _sigmoid(x):
    return jax.nn.sigmoid(x)

def _layernorm(x, axis=-1, eps=1e-05):
    m = jnp.mean(x, axis=axis, keepdims=True)
    v = jnp.var(x, axis=axis, keepdims=True)
    return (x - m) / jnp.sqrt(v + eps)

def _scatter_add(tgt, idx, src, axis=0):
    return tgt.at[idx].add(src)

def _segment_sum(src, seg, n):
    return jax.ops.segment_sum(src, seg, n)
kernel_name = 'mk_xattn_ffn_d1_seqx_r8_74af0e'

def setup_inputs(seed: int=0):
    np.random.seed(seed)
    _w = jnp.asarray

    def _rec_inputs():
        import jax
        import jax.numpy as jnp
        _rk = jax.random.key(seed)
        x = -0.000125 + 0.9999 * jax.random.normal(jax.random.fold_in(_rk, 1), (4, 512, 128), jnp.float32)
        _lenS = 512 - jax.random.randint(jax.random.fold_in(_rk, 7), (4,), 0, max(1, 512 // 4) + 1, jnp.int32)
        _lenS2 = 77 - jax.random.randint(jax.random.fold_in(_rk, 8), (4,), 0, max(1, 77 // 4) + 1, jnp.int32)
        _ctx_768P = jax.random.normal(jax.random.fold_in(_rk, 11), (4, 16, 96), jnp.float32)
        _ctx_768c = jax.random.dirichlet(jax.random.fold_in(_rk, 511), 0.3 * jnp.ones((16,), jnp.float32), (4, 77))
        _ctx_768t = jnp.einsum('bsk,bkd->bsd', _ctx_768c, _ctx_768P)
        _ctx_768t = _ctx_768t * jax.lax.rsqrt(jnp.mean(jnp.square(_ctx_768t)) + 1e-12) * 0.953939
        ctx_768 = 0.00272024 + 0.999456 * (_ctx_768t + 0.3 * jax.random.normal(jax.random.fold_in(_rk, 611), (4, 77, 96), jnp.float32))
        return (x, ctx_768)
    x, ctx_768 = _rec_inputs()

    def _L0_xattn_setup():
        import jax, jax.numpy as jnp
        import numpy as np
        N_HEADS = 16
        DIM_EMBED = 128
        DIM_CROSS = 96
        DIM_HEAD = DIM_EMBED // N_HEADS
        key = jax.random.key(seed)
        ks = jax.random.split(key, 10)
        B, Sq, Sk = (8, 512, 77)
        s_e = 1.0 / np.sqrt(DIM_EMBED)
        s_c = 1.0 / np.sqrt(DIM_CROSS)
        return {'x': jax.random.normal(ks[0], (B, Sq, DIM_EMBED), jnp.float32), 'y': jax.random.normal(ks[1], (B, Sk, DIM_CROSS), jnp.float32), 'wq': jax.random.normal(ks[2], (DIM_EMBED, DIM_EMBED), jnp.float32) * s_e, 'bq': jax.random.normal(ks[3], (DIM_EMBED,), jnp.float32) * 0.01, 'wk': jax.random.normal(ks[4], (DIM_CROSS, DIM_EMBED), jnp.float32) * s_c, 'bk': jax.random.normal(ks[5], (DIM_EMBED,), jnp.float32) * 0.01, 'wv': jax.random.normal(ks[6], (DIM_CROSS, DIM_EMBED), jnp.float32) * s_c, 'bv': jax.random.normal(ks[7], (DIM_EMBED,), jnp.float32) * 0.01, 'wo': jax.random.normal(ks[8], (DIM_EMBED, DIM_EMBED), jnp.float32) * s_e, 'bo': jax.random.normal(ks[9], (DIM_EMBED,), jnp.float32) * 0.01}
    _L0_xattn_all = _L0_xattn_setup()
    _L0_xattn_in = {k: v for k, v in _L0_xattn_all.items() if k in ('wq', 'bq', 'wk', 'bk', 'wv', 'bv', 'wo', 'bo')}
    del _L0_xattn_all

    def _L0_ffn_setup():
        import jax, jax.numpy as jnp
        import numpy as np
        DIM = 128
        EXPERT_DIM = 64
        N_EXPERTS = 16
        TOPK = 2
        SHARED_HIDDEN = EXPERT_DIM * TOPK
        B, T = (4, 128)

        def _moe_forward(x, router_w, router_bias, up_proj, gate_proj, down_proj, sh_gate, sh_up, sh_down):
            Bb, Tt, D = x.shape
            flat = x.reshape(Bb * Tt, D)
            N = flat.shape[0]
            logits = flat @ router_w.T
            topk_scores, topk_idx = jax.lax.top_k(logits + router_bias, TOPK)
            topk_scores = jax.nn.softmax(topk_scores, axis=-1)
            combine = jnp.zeros((N, N_EXPERTS), flat.dtype)
            combine = combine.at[jnp.arange(N)[:, None], topk_idx].add(topk_scores)
            up_all = jnp.einsum('nd,kde->nke', flat, up_proj)
            gate_all = jnp.einsum('nd,kde->nke', flat, gate_proj)
            hidden = jax.nn.silu(gate_all) * up_all
            down_all = jnp.einsum('nke,ked->nkd', hidden, down_proj)
            out = jnp.einsum('nk,nkd->nd', combine, down_all)
            sh_hidden = jax.nn.silu(flat @ sh_gate.T) * (flat @ sh_up.T)
            out = out + sh_hidden @ sh_down.T
            return out.reshape(Bb, Tt, D)
        key = jax.random.key(seed)
        ks = jax.random.split(key, 9)
        std = 0.02
        return {'x': jax.random.normal(ks[0], (B, T, DIM), jnp.float32), 'router_w': jax.random.normal(ks[1], (N_EXPERTS, DIM), jnp.float32) * std, 'router_bias': jnp.zeros((N_EXPERTS,), jnp.float32), 'up_proj': jax.random.normal(ks[2], (N_EXPERTS, DIM, EXPERT_DIM), jnp.float32) * std, 'gate_proj': jax.random.normal(ks[3], (N_EXPERTS, DIM, EXPERT_DIM), jnp.float32) * std, 'down_proj': jax.random.normal(ks[4], (N_EXPERTS, EXPERT_DIM, DIM), jnp.float32) * std, 'sh_gate': jax.random.normal(ks[5], (SHARED_HIDDEN, DIM), jnp.float32) * std, 'sh_up': jax.random.normal(ks[6], (SHARED_HIDDEN, DIM), jnp.float32) * std, 'sh_down': jax.random.normal(ks[7], (DIM, SHARED_HIDDEN), jnp.float32) * std}
    _L0_ffn_all = _L0_ffn_setup()
    _L0_ffn_in = {k: v for k, v in _L0_ffn_all.items() if k in ('router_w', 'router_bias', 'up_proj', 'gate_proj', 'down_proj', 'sh_gate', 'sh_up', 'sh_down')}
    del _L0_ffn_all
    return {'x': x, 'ctx_768': ctx_768, 'L0_xattn_wq': _L0_xattn_in['wq'], 'L0_xattn_bq': _L0_xattn_in['bq'], 'L0_xattn_wk': _L0_xattn_in['wk'], 'L0_xattn_bk': _L0_xattn_in['bk'], 'L0_xattn_wv': _L0_xattn_in['wv'], 'L0_xattn_bv': _L0_xattn_in['bv'], 'L0_xattn_wo': _L0_xattn_in['wo'], 'L0_xattn_bo': _L0_xattn_in['bo'], 'L0_ffn_router_w': _L0_ffn_in['router_w'], 'L0_ffn_router_bias': _L0_ffn_in['router_bias'], 'L0_ffn_up_proj': _L0_ffn_in['up_proj'], 'L0_ffn_gate_proj': _L0_ffn_in['gate_proj'], 'L0_ffn_down_proj': _L0_ffn_in['down_proj'], 'L0_ffn_sh_gate': _L0_ffn_in['sh_gate'], 'L0_ffn_sh_up': _L0_ffn_in['sh_up'], 'L0_ffn_sh_down': _L0_ffn_in['sh_down']}

def reference(x, ctx_768, L0_xattn_wq, L0_xattn_bq, L0_xattn_wk, L0_xattn_bk, L0_xattn_wv, L0_xattn_bv, L0_xattn_wo, L0_xattn_bo, L0_ffn_router_w, L0_ffn_router_bias, L0_ffn_up_proj, L0_ffn_gate_proj, L0_ffn_down_proj, L0_ffn_sh_gate, L0_ffn_sh_up, L0_ffn_sh_down):
    import jax
    import jax.numpy as jnp

    def _L0_xattn_ref(x, y, wq, bq, wk, bk, wv, bv, wo, bo):
        import jax, jax.numpy as jnp
        import numpy as np
        N_HEADS = 16
        DIM_EMBED = 128
        DIM_CROSS = 96
        DIM_HEAD = DIM_EMBED // N_HEADS
        B, Sq, E = x.shape
        H, D = (N_HEADS, DIM_HEAD)
        q = (x @ wq + bq).reshape(B, Sq, H, D).transpose(0, 2, 1, 3)
        k = (y @ wk + bk).reshape(B, -1, H, D).transpose(0, 2, 1, 3)
        v = (y @ wv + bv).reshape(B, -1, H, D).transpose(0, 2, 1, 3)
        scores = jnp.einsum('bhqd,bhkd->bhqk', q, k) / jnp.sqrt(jnp.asarray(D, x.dtype))
        attn = jax.nn.softmax(scores, axis=-1)
        out = jnp.einsum('bhqk,bhkd->bhqd', attn, v)
        out = out.transpose(0, 2, 1, 3).reshape(B, Sq, E)
        return out @ wo + bo

    def _L0_ffn_ref(x, router_w, router_bias, up_proj, gate_proj, down_proj, sh_gate, sh_up, sh_down):
        import jax, jax.numpy as jnp
        import numpy as np
        DIM = 128
        EXPERT_DIM = 64
        N_EXPERTS = 16
        TOPK = 2
        SHARED_HIDDEN = EXPERT_DIM * TOPK
        B, T = (4, 128)

        def _moe_forward(x, router_w, router_bias, up_proj, gate_proj, down_proj, sh_gate, sh_up, sh_down):
            Bb, Tt, D = x.shape
            flat = x.reshape(Bb * Tt, D)
            N = flat.shape[0]
            logits = flat @ router_w.T
            topk_scores, topk_idx = jax.lax.top_k(logits + router_bias, TOPK)
            topk_scores = jax.nn.softmax(topk_scores, axis=-1)
            combine = jnp.zeros((N, N_EXPERTS), flat.dtype)
            combine = combine.at[jnp.arange(N)[:, None], topk_idx].add(topk_scores)
            up_all = jnp.einsum('nd,kde->nke', flat, up_proj)
            gate_all = jnp.einsum('nd,kde->nke', flat, gate_proj)
            hidden = jax.nn.silu(gate_all) * up_all
            down_all = jnp.einsum('nke,ked->nkd', hidden, down_proj)
            out = jnp.einsum('nk,nkd->nd', combine, down_all)
            sh_hidden = jax.nn.silu(flat @ sh_gate.T) * (flat @ sh_up.T)
            out = out + sh_hidden @ sh_down.T
            return out.reshape(Bb, Tt, D)
        return _moe_forward(x, router_w, router_bias, up_proj, gate_proj, down_proj, sh_gate, sh_up, sh_down)
    x = x + _L0_xattn_ref(_layernorm(x, axis=-1), ctx_768, L0_xattn_wq, L0_xattn_bq, L0_xattn_wk, L0_xattn_bk, L0_xattn_wv, L0_xattn_bv, L0_xattn_wo, L0_xattn_bo)
    x = x + _L0_ffn_ref(_layernorm(x, axis=-1), L0_ffn_router_w, L0_ffn_router_bias, L0_ffn_up_proj, L0_ffn_gate_proj, L0_ffn_down_proj, L0_ffn_sh_gate, L0_ffn_sh_up, L0_ffn_sh_down)
    return x

_drawn_inputs = setup_inputs


def setup_inputs(seed=0):
    import zlib

    import numpy as np

    out = dict(_drawn_inputs(seed))
    spreads = {'L0_ffn_router_bias': (0.0, 0.8)}
    factors = {'L0_xattn_bq': 8.0,
     'L0_xattn_bk': 8.0,
     'L0_xattn_bv': 6.443,
     'L0_xattn_bo': 5.852,
     'L0_ffn_router_w': 8.0,
     'L0_ffn_up_proj': 8.0,
     'L0_ffn_gate_proj': 8.0,
     'L0_ffn_down_proj': 8.0,
     'L0_ffn_sh_gate': 8.0,
     'L0_ffn_sh_up': 8.0,
     'L0_ffn_sh_down': 8.0}
    for name, (base, spread) in spreads.items():
        noise = np.random.default_rng([zlib.crc32(name.encode()), seed]).standard_normal(out[name].shape)
        drawn = base * np.exp(spread * noise) if base else spread * noise
        out[name] = jnp.asarray(drawn.astype(out[name].dtype))
    for name, factor in factors.items():
        out[name] = (out[name] * factor).astype(out[name].dtype)
    return out
```

```python
from contextlib import ExitStack

import concourse.bass as bass
from concourse import mybir

F32 = mybir.dt.float32
F32R = mybir.dt.float32r
U32 = mybir.dt.uint32
ALU = mybir.AluOpType
ACT = mybir.ActivationFunctionType
AX = mybir.AxisListType

P = 128
QUAD = 32
EPS = 1e-5


def build(nc, x, ctx_t, wq, bq, wk, wv, wo, bo, router_t, router_bias, up, gate, down,
          sh_gate_t, sh_up_t, sh_down_t, consts, out):
    B, S, D = x.shape
    H, HD = 16, D // 16
    G, HG = 4, 4
    SK = ctx_t.shape[2]
    C1 = ctx_t.shape[0]
    GK = HG * SK
    KC = [(0, 104), (104, 206), (206, 308)]
    NJ = len(KC)
    T = S // P
    E, _, F = up.shape
    NP = E // 2
    NU = NP + 1
    SCALE = float(HD) ** -0.5
    assert D == P and GK == KC[-1][1] and 2 * F == P and HG * HD == QUAD

    ctx = ExitStack()
    with ctx:
        def sb(name, shape, dt=F32):
            return ctx.enter_context(nc.sbuf_tensor(name, shape, dt))

        def sem(name):
            return ctx.enter_context(nc.semaphore(name))

        x_sb = sb("x_sb", [P, B, T, D])
        x_bo = sb("x_bo", [P, B, T, D])
        x2 = sb("x2", [P, B, T, D])
        ctx_sb = sb("ctx_sb", [C1, B, SK])
        ctx_rep = sb("ctx_rep", [C1, B, HG, SK])
        cst = sb("cst", [P, consts.shape[1]])
        ident = cst[:, 0:P]
        k_mask = cst[:, P:P + G * HG].rearrange("p (g h) -> p g h", g=G)
        v_mask = cst[:, P + 16:P + 16 + NJ * P].rearrange("p (j n) -> p j n", j=NJ)
        pair_rows = cst[:, P + 16 + NJ * P:P + 32 + NJ * P]
        iota = cst[:, P + 32 + NJ * P:P + 48 + NJ * P]
        wq_sb = sb("wq_sb", [P, G, P])
        wq_hi = sb("wq_hi", [P, G, P], F32R)
        wq_lo = sb("wq_lo", [P, G, P], F32R)
        bq_sb = sb("bq_sb", [P, G])
        wk_sb = sb("wk_sb", [C1, G, P])
        wv_sb = sb("wv_sb", [C1, D])
        wo_sb = sb("wo_sb", [P, D])
        bo_sb = sb("bo_sb", [P, D])
        rw_sb = sb("rw_sb", [P, E])
        rw_st = sb("rw_st", [P, 2, E], F32R)
        rb_sb = sb("rb_sb", [P, E])
        wg_sb = sb("wg_sb", [P, NU, P])
        wu_sb = sb("wu_sb", [P, NU, P])
        wg_hi = sb("wg_hi", [P, NU, P], F32R)
        wg_lo = sb("wg_lo", [P, NU, P], F32R)
        wu_hi = sb("wu_hi", [P, NU, P], F32R)
        wu_lo = sb("wu_lo", [P, NU, P], F32R)
        wd_sb = sb("wd_sb", [P, NU, D])
        sel = sb("sel", [P, E, F], F32R)

        k_st = sb("k_st", [P, G, B * SK], F32R)
        k_bd = sb("k_bd", [P, G, B, GK], F32R)
        v_bd = sb("v_bd", [P, B, NJ, D])
        stats = sb("stats", [P, T, 6])
        mean_var = sb("mean_var", [P, 2, T, 2])
        var_eps = sb("var_eps", [P, 2, T])
        rstd = sb("rstd", [P, 2, T])
        minus_half = sb("minus_half", [P, T])
        xn = sb("xn", [P, 2, T, D])
        xt_hi = sb("xt_hi", [P, S], F32R)
        xt_lo = sb("xt_lo", [P, S], F32R)
        q_st = sb("q_st", [P, 2, G, S], F32R)
        neg_max = sb("neg_max", [P, T, H])
        max_st = sb("max_st", [P, T, P], F32R)
        probs = sb("probs", [P, 8, S])
        den_sb = sb("den_sb", [P, S])
        den_inv = sb("den_inv", [P, T, H])
        den_rep = sb("den_rep", [P, T, D])
        inv_t = sb("inv_t", [P, S])
        att_t = sb("att_t", [P, S])
        x2t_hi = sb("x2t_hi", [P, B * S], F32R)
        x2t_lo = sb("x2t_lo", [P, B * S], F32R)
        logits = sb("logits", [P, T, E])
        top_v = sb("top_v", [P, T, 8])
        top_i = sb("top_i", [P, T, 8], U32)
        top_f = sb("top_f", [P, T, 2])
        gap = sb("gap", [P, T])
        gap_exp = sb("gap_exp", [P, T])
        gap_sum = sb("gap_sum", [P, T])
        top_w = sb("top_w", [P, T, 2])
        picked = sb("picked", [P, T, 2, E])
        combine = sb("combine", [P, T, E])
        comb_st = sb("comb_st", [P, T, P], F32R)
        comb_t = sb("comb_t", [P, B * S], F32R)
        silu = sb("silu", [P, 2, S])
        hid_u = sb("hid_u", [P, 2, S])
        hid = sb("hid", [P, 3, S])
        y_sb = sb("y_sb", [P, 2, T, D])

        banks = [ctx.enter_context(nc.psum_tensor(f"bank{i}", [P, 512], F32)) for i in range(8)]
        misc = banks[0:2]
        sq_ps = banks[2:4]
        st_ps = banks[4:6]
        po, pd = banks[6], banks[7]
        gate_ps, up_ps, comb_ps, acc_ps = banks[0:2], banks[2:4], banks[4:6], banks[6:8]

        names = ("consts", "ctx", "wk", "wv", "wq", "bq", "wo", "bo", "rw", "rb", "wgu", "wd")
        ld = {n: sem(f"ld_{n}") for n in names}
        ld_x = [sem(f"ld_x{b}") for b in range(B)]
        misc_ready = [sem("misc0_ready"), sem("misc1_ready")]
        dve_step = sem("dve_step")
        pool_step = sem("pool_step")
        zeroed = sem("zeroed")
        ctx_rep_ready = sem("ctx_rep_ready")
        wq_split = sem("wq_split")
        rw_split = sem("rw_split")
        k_hi_ready = sem("k_hi_ready")
        k_st_ready = sem("k_st_ready")
        k_bd_ready = sem("k_bd_ready")
        v_bd_ready = sem("v_bd_ready")
        stats_ready = [sem("stats1_ready"), sem("stats2_ready")]
        xn_ready = [sem("xn1_ready"), sem("xn2_ready")]
        x_bo_ready = sem("x_bo_ready")
        xt_hi_ready = sem("xt_hi_ready")
        xt_lo_ready = sem("xt_lo_ready")
        q_hi_ready = sem("q_hi_ready")
        q_lo_ready = sem("q_lo_ready")
        sq_ready = sem("sq_ready")
        max_done = sem("max_done")
        max_st_ready = sem("max_st_ready")
        q_max_ready = sem("q_max_ready")
        st_ready = sem("st_ready")
        exp_done = sem("exp_done")
        pv_done = sem("pv_done")
        den_copied = sem("den_copied")
        den_inv_ready = sem("den_inv_ready")
        den_rep_ready = sem("den_rep_ready")
        inv_t_ready = sem("inv_t_ready")
        att_ready = sem("att_ready")
        x2_ready = sem("x2_ready")
        x2t_hi_ready = sem("x2t_hi_ready")
        x2t_lo_ready = sem("x2t_lo_ready")
        router_read = sem("router_read")
        gap_ready = sem("gap_ready")
        gap_exp_ready = sem("gap_exp_ready")
        comb_st_ready = sem("comb_st_ready")
        comb_t_ready = sem("comb_t_ready")
        w_hi_ready = sem("w_hi_ready")
        w_lo_ready = sem("w_lo_ready")
        sel_ready = sem("sel_ready")
        gate_ready = sem("gate_ready")
        up_ready = sem("up_ready")
        comb_ready = sem("comb_ready")
        silu_done = sem("silu_done")
        hid_u_done = sem("hid_u_done")
        hid_ready = sem("hid_ready")
        down_done = sem("down_done")
        y_ready = sem("y_ready")
        out_done = [sem("out_done_even"), sem("out_done_odd")]

        uses = [("k", g) for g in range(G)] + [("v", b) for b in range(B)]
        for i in range(B + 3):
            if 0 <= i - 3 < B:
                uses.append(("comb", i - 3))
            if 0 <= i - 2 < B:
                uses.append(("den", i - 2))
            if i < B:
                uses.append(("xt", i))
                uses += [("q", i, g) for g in range(G)]
            if 0 <= i - 2 < B:
                uses.append(("inv", i - 2))
                uses.append(("wo", i - 2))
                uses.append(("x2t", i - 2))
            if i < B:
                uses.append(("max", i))
            if 0 <= i - 2 < B:
                uses.append(("router", i - 2))
        turn = {u: n for n, u in enumerate(uses)}

        def misc_of(*use):
            n = turn[use]
            return n % 2, n // 2 + 1

        def released(kind, i, g=0):
            return {"k": (k_st_ready, i + 1), "v": (v_bd_ready, i + 1), "comb": (comb_t_ready, i + 1),
                    "den": (den_inv_ready, i + 1), "xt": (xt_lo_ready, i + 1), "q": (q_lo_ready, i * G + g + 1),
                    "inv": (inv_t_ready, i + 1), "wo": (x2_ready, i + 1), "x2t": (x2t_lo_ready, i + 1),
                    "max": (q_max_ready, (i + 1) * G), "router": (router_read, i + 1)}[kind]

        def gate_read(u):
            return silu_done, u + 1

        def up_read(u):
            n, p = u // NU, u % NU
            return (hid_u_done, n * NP + p + 1) if p < NP else (hid_ready, u + 1)

        def quads(g):
            return [a for a in range(4) if a != g]

        block = ctx.enter_context(nc.Block())

        @block.sync
        def _(sp):
            sp.dma_start(x_sb[:, 0], x[0].rearrange("(t p) d -> p t d", p=P)).then_inc(ld_x[0], 16)
            sp.dma_start(ctx_sb[:], ctx_t).then_inc(ld["ctx"], 16)
            sp.dma_start(wk_sb[:], wk).then_inc(ld["wk"], 16)
            sp.dma_start(cst[:], consts).then_inc(ld["consts"], 16)
            sp.dma_start(wq_sb[:], wq).then_inc(ld["wq"], 16)
            sp.dma_start(bq_sb[:], bq).then_inc(ld["bq"], 16)
            sp.dma_start(wv_sb[:], wv).then_inc(ld["wv"], 16)
            for b in range(1, B):
                sp.dma_start(x_sb[:, b], x[b].rearrange("(t p) d -> p t d", p=P)).then_inc(ld_x[b], 16)
            sp.dma_start(bo_sb[:], bo.partition_broadcast(P)).then_inc(ld["bo"], 16)
            sp.dma_start(wo_sb[:], wo).then_inc(ld["wo"], 16)
            sp.dma_start(rw_sb[:], router_t).then_inc(ld["rw"], 16)
            sp.dma_start(rb_sb[:], router_bias.partition_broadcast(P)).then_inc(ld["rb"], 16)
            sp.dma_start(wg_sb[:, 0:NP, :].rearrange("p n (a f) -> p (n a) f", a=2),
                         gate.rearrange("e d f -> d e f")).then_inc(ld["wgu"], 16)
            sp.dma_start(wg_sb[:, NP, :], sh_gate_t).then_inc(ld["wgu"], 16)
            sp.dma_start(wu_sb[:, 0:NP, :].rearrange("p n (a f) -> p (n a) f", a=2),
                         up.rearrange("e d f -> d e f")).then_inc(ld["wgu"], 16)
            sp.dma_start(wu_sb[:, NP, :], sh_up_t).then_inc(ld["wgu"], 16)
            sp.dma_start(wd_sb[:, 0:NP, :], down.rearrange("(n a) f d -> (a f) n d", a=2)).then_inc(ld["wd"], 16)
            sp.dma_start(wd_sb[:, NP, :], sh_down_t).then_inc(ld["wd"], 16)
            for n in range(B):
                sp.wait_ge(y_ready, n + 1)
                sp.dma_start(out[n].rearrange("(t p) d -> p t d", p=P), y_sb[:, n % 2])\
                    .then_inc(out_done[n % 2], 16)
            sp.wait_ge(out_done[0], 16 * (B // 2))
            sp.wait_ge(out_done[1], 16 * (B // 2))

        @block.gpsimd
        def _(pool):
            steps = [0]

            def chain(ins):
                ins.then_inc(pool_step, 1)
                steps[0] += 1
                pool.wait_ge(pool_step, steps[0])

            def norm(which, n, src):
                pool.wait_ge(stats_ready[which], n + 1)
                chain(nc.gpsimd.tensor_scalar(var_eps[:, which], mean_var[:, which, :, 1], EPS, None, ALU.add))
                chain(nc.gpsimd.tensor_tensor(rstd[:, which], var_eps[:, which], minus_half[:], ALU.pow))
                if n > 0:
                    k, turns = misc_of(("xt", "x2t")[which], n - 1)
                    pool.wait_ge(misc_ready[k], turns)
                for t in range(T):
                    last = nc.gpsimd.tensor_scalar(xn[:, which, t], src[:, n, t], mean_var[:, which, t, 0:1],
                                                   rstd[:, which, t:t + 1], ALU.subtract, ALU.mult)
                last.then_inc(xn_ready[which], 1)

            def expand_k(b):
                for g in range(G):
                    if b == 0:
                        pool.wait_ge(k_st_ready, g + 1)
                    keys = k_st[:, g, b * SK:(b + 1) * SK].bitcast(F32)
                    nc.gpsimd.tensor_tensor(
                        k_bd[:, g, b].rearrange("p (h k) -> p h k", h=HG),
                        keys.unsqueeze(1).to_broadcast([P, HG, SK]),
                        k_mask[:, g].unsqueeze(2).to_broadcast([P, HG, SK]), ALU.mult).then_inc(k_bd_ready, 1)

            nc.gpsimd.memset(minus_half[:], -0.5).then_inc(zeroed, 1)
            nc.gpsimd.memset(max_st[:].bitcast(F32), 0.0).then_inc(zeroed, 1)
            nc.gpsimd.memset(comb_st[:].bitcast(F32), 0.0).then_inc(zeroed, 1)
            pool.wait_ge(zeroed, 3)
            norm(0, 0, x_sb)
            pool.wait_ge(ld["consts"], 16)
            expand_k(0)
            pool.wait_ge(ld["ctx"], 16)
            for b in range(B):
                last = nc.gpsimd.tensor_copy(ctx_rep[:, b], ctx_sb[:, b].unsqueeze(1).to_broadcast([C1, HG, SK]))
            last.then_inc(ctx_rep_ready, 1)
            norm(0, 1, x_sb)
            expand_k(1)
            nc.gpsimd.tensor_copy(sel[:], pair_rows.unsqueeze(2).to_broadcast([P, E, F])).then_inc(sel_ready, 1)
            pool.wait_ge(ld["bo"], 16)
            for i in range(2, B + 2):
                b = i - 2
                if i < B:
                    norm(0, i, x_sb)
                nc.gpsimd.tensor_tensor(x_bo[:, b], x_sb[:, b], bo_sb[:].unsqueeze(1).to_broadcast([P, T, D]),
                                        ALU.add).then_inc(x_bo_ready, 1)
                pool.wait_ge(den_inv_ready, b + 1)
                if b > 0:
                    pool.wait_ge(misc_ready[misc_of("inv", b - 1)[0]], misc_of("inv", b - 1)[1])
                nc.gpsimd.tensor_copy(den_rep[:, :].rearrange("p t (h d) -> p (t h) d", d=HD),
                                      den_inv[:].rearrange("p t h -> p (t h)").unsqueeze(2)
                                      .to_broadcast([P, T * H, HD])).then_inc(den_rep_ready, 1)
                if i < B:
                    expand_k(i)
                if i == 2:
                    pool.wait_ge(w_hi_ready, 2)
                    nc.gpsimd.tensor_tensor(wg_lo[:], wg_sb[:], wg_hi[:].bitcast(F32), ALU.subtract)\
                        .then_inc(w_lo_ready, 1)
                norm(1, b, x2)
                if i == 3:
                    nc.gpsimd.tensor_tensor(wu_lo[:], wu_sb[:], wu_hi[:].bitcast(F32), ALU.subtract)\
                        .then_inc(w_lo_ready, 1)

        @block.scalar
        def _(act):
            def copy_misc(dst, rows, use, done):
                k, n = misc_of(*use)
                act.wait_ge(misc_ready[k], n)
                nc.scalar.activation(dst, misc[k][rows, 0:dst.shape[-1]], ACT.Copy).then_inc(done, 1)

            for g in range(G):
                copy_misc(k_st[:, g], slice(0, P), ("k", g), k_hi_ready)
            for i in range(B + 3):
                if 0 <= i - 3 < B:
                    copy_misc(comb_t[:, (i - 3) * S:(i - 2) * S], slice(0, P), ("comb", i - 3), comb_t_ready)
                if i < B:
                    copy_misc(xt_hi[:], slice(0, P), ("xt", i), xt_hi_ready)
                    if i == 0:
                        act.wait_ge(ld["bq"], 16)
                    for g in range(G):
                        k, n = misc_of("q", i, g)
                        act.wait_ge(misc_ready[k], n)
                        nc.scalar.activation(q_st[:, i % 2, g], misc[k][:, 0:S], ACT.Identity,
                                             bias=bq_sb[:, g:g + 1]).then_inc(q_hi_ready, 1)
                if 0 <= i - 2 < B:
                    copy_misc(inv_t[:], slice(0, P), ("inv", i - 2), inv_t_ready)
                if 0 <= i - 1 < B:
                    for m in range(NJ * G):
                        e = (i - 1) * NJ * G + m
                        rows = KC[m // G][1] - KC[m // G][0]
                        act.wait_ge(st_ready, e + 1)
                        if e >= 8:
                            act.wait_ge(pv_done, (e - 8) // G + 1)
                        nc.scalar.activation(probs[0:rows, e % 8], st_ps[e % 2][0:rows, :], ACT.Exp,
                                             scale=SCALE).then_inc(exp_done, 1)
                if i == 1:
                    act.wait_ge(ld["wgu"], 64)
                    nc.scalar.activation(wg_hi[:], wg_sb[:], ACT.Copy).then_inc(w_hi_ready, 1)
                    nc.scalar.activation(wu_hi[:], wu_sb[:], ACT.Copy).then_inc(w_hi_ready, 1)
                if 0 <= i - 2 < B:
                    copy_misc(x2t_hi[:, (i - 2) * S:(i - 1) * S], slice(0, P), ("x2t", i - 2), x2t_hi_ready)
                if i < B:
                    k, n = misc_of("max", i)
                    act.wait_ge(misc_ready[k], n)
                    for g in range(G):
                        a = slice(QUAD * g, QUAD * (g + 1))
                        nc.scalar.activation(q_st[a, i % 2, g], misc[k][a, 0:S], ACT.Copy)\
                            .then_inc(q_max_ready, 1)
                if 0 <= i - 1 < B:
                    act.wait_ge(pv_done, NJ * i)
                    nc.scalar.activation(den_sb[:], pd[:], ACT.Copy).then_inc(den_copied, 1)
                if 0 <= i - 2 < B:
                    act.wait_ge(gap_ready, i - 1)
                    nc.scalar.activation(gap_exp[:], gap[:], ACT.Exp).then_inc(gap_exp_ready, 1)
            for n in range(B):
                for p in range(NU):
                    u = n * NU + p
                    act.wait_ge(gate_ready, u + 1)
                    if u >= 2:
                        act.wait_ge(*up_read(u - 2))
                    nc.scalar.activation(silu[:, u % 2], gate_ps[u % 2][:], ACT.Silu).then_inc(silu_done, 1)

        @block.vector
        def _(dve):
            steps = [0]

            def chain(ins):
                ins.then_inc(dve_step, 1)
                steps[0] += 1
                dve.wait_ge(dve_step, steps[0])

            def moments(which, n, src):
                for t in range(T):
                    ins = nc.vector.bn_stats(stats[:, t], src[:, n, t])
                chain(ins)
                if n > 0:
                    dve.wait_ge(xn_ready[which], n)
                for t in range(T):
                    last = nc.vector.bn_aggr(mean_var[:, which, t], stats[:, t])
                last.then_inc(stats_ready[which], 1)

            def low_part(dst, src, hi, use, hi_ready, hi_count, done):
                k, n = misc_of(*use)
                dve.wait_ge(hi_ready, hi_count)
                nc.vector.tensor_tensor(dst, src(misc[k]), hi.bitcast(F32), ALU.subtract).then_inc(done, 1)

            dve.wait_ge(ld_x[0], 16)
            moments(0, 0, x_sb)
            for g in range(G):
                k, n = misc_of("k", g)
                a = slice(QUAD * quads(g)[2], QUAD * quads(g)[2] + QUAD)
                dve.wait_ge(k_hi_ready, g + 1)
                ins = nc.vector.tensor_tensor(k_st[a, g], misc[k][a, 0:B * SK], k_st[a, g].bitcast(F32), ALU.subtract)
                ins.then_inc(k_st_ready, 1)
            dve.wait_ge(ld["wq"], 16)
            chain(nc.vector.tensor_copy(wq_hi[:], wq_sb[:]))
            nc.vector.tensor_tensor(wq_lo[:], wq_sb[:], wq_hi[:].bitcast(F32), ALU.subtract).then_inc(wq_split, 1)
            dve.wait_ge(ld_x[1], 16)
            moments(0, 1, x_sb)
            dve.wait_ge(ld["consts"], 16)
            for b in range(B):
                k, n = misc_of("v", b)
                dve.wait_ge(misc_ready[k], n)
                for j, (a, z) in enumerate(KC):
                    ins = nc.vector.tensor_tensor(v_bd[0:z - a, b, j], misc[k][0:z - a, j * D:(j + 1) * D],
                                                  v_mask[0:z - a, j], ALU.mult)
                ins.then_inc(v_bd_ready, 1)
            dve.wait_ge(ld["rw"], 16)
            chain(nc.vector.tensor_copy(rw_st[:, 0], rw_sb[:]))
            nc.vector.tensor_tensor(rw_st[:, 1], rw_sb[:], rw_st[:, 0].bitcast(F32), ALU.subtract)\
                .then_inc(rw_split, 1)
            dve.wait_ge(zeroed, 3)
            dve.wait_ge(ld["rb"], 16)

            for i in range(B + 3):
                b = i - 2
                if 0 <= b < B:
                    k, n = misc_of("den", b)
                    dve.wait_ge(misc_ready[k], n)
                    if b > 0:
                        dve.wait_ge(den_rep_ready, b)
                    ins = nc.vector.reciprocal(den_inv[:].rearrange("p t h -> p (t h)"),
                                               misc[k][:].rearrange("p (n d) -> p n d", d=HD)[:, :, 0])
                    ins.then_inc(den_inv_ready, 1)
                if i < B:
                    low_part(xt_lo[:], lambda ps: ps[:, 0:S], xt_hi[:], ("xt", i), xt_hi_ready, i + 1, xt_lo_ready)
                    for g in range(G):
                        k, n = misc_of("q", i, g)
                        a = slice(QUAD * quads(g)[1], QUAD * quads(g)[1] + QUAD)
                        dve.wait_ge(q_hi_ready, i * G + g + 1)
                        ins = nc.vector.scalar_tensor_tensor(
                            out=q_st[a, i % 2, g], in0=misc[k][a, 0:S], scalar=bq_sb[a, g:g + 1],
                            in1=q_st[a, i % 2, g].bitcast(F32), op0=ALU.add, op1=ALU.subtract)
                        ins.then_inc(q_lo_ready, 1)
                if 0 <= b < B:
                    dve.wait_ge(inv_t_ready, b + 1)
                    nc.vector.tensor_tensor(att_t[:], po[:], inv_t[:], ALU.mult).then_inc(att_ready, 1)
                for m in range(T * G):
                    if i < B:
                        t, g = m // G, m % G
                        w = i * T * G + m
                        dve.wait_ge(sq_ready, w + 1)
                        ins = nc.vector.tensor_reduce(
                            neg_max[:, t, g * HG:(g + 1) * HG],
                            sq_ps[w % 2][:, 0:GK].rearrange("p (h k) -> p h k", h=HG), AX.X, ALU.max, negate=True)
                        ins.then_inc(max_done, 1)
                    if m == 7 and 0 <= b < B:
                        k, n = misc_of("wo", b)
                        dve.wait_ge(misc_ready[k], n)
                        dve.wait_ge(x_bo_ready, b + 1)
                        ins = nc.vector.tensor_tensor(x2[:, b].rearrange("p t d -> p (t d)"), misc[k][:],
                                                      x_bo[:, b].rearrange("p t d -> p (t d)"), ALU.add)
                        ins.then_inc(x2_ready, 1)
                        dve.wait_ge(x2_ready, b + 1)
                        moments(1, b, x2)
                if i < B:
                    dve.wait_ge(max_done, (i + 1) * T * G)
                    if i > 0:
                        k, n = misc_of("max", i - 1)
                        dve.wait_ge(misc_ready[k], n)
                    heads = neg_max[:].rearrange("p t (g h) -> p t g h", g=G)
                    placed = max_st[:].rearrange("p t (g c) -> p t g c", g=G)
                    chain(nc.vector.tensor_copy(placed[:, :, :, 0:HG], heads))
                    nc.vector.tensor_tensor(placed[:, :, :, HG:2 * HG], heads, placed[:, :, :, 0:HG].bitcast(F32),
                                            ALU.subtract).then_inc(max_st_ready, 1)
                if 0 <= b < B:
                    low_part(x2t_lo[:, b * S:(b + 1) * S], lambda ps: ps[:, 0:S], x2t_hi[:, b * S:(b + 1) * S],
                             ("x2t", b), x2t_hi_ready, b + 1, x2t_lo_ready)
                if 1 <= i < B - 1:
                    dve.wait_ge(ld_x[i + 1], 16)
                    moments(0, i + 1, x_sb)
                if 0 <= b < B:
                    k, n = misc_of("router", b)
                    dve.wait_ge(misc_ready[k], n)
                    parts = misc[k][:, 0:T * 2 * E].rearrange("p (t a e) -> p t a e", a=2, e=E)
                    chain(nc.vector.tensor_tensor(logits[:], parts[:, :, 0], rb_sb[:].unsqueeze(1)
                                                  .to_broadcast([P, T, E]), ALU.add))
                    nc.vector.tensor_tensor(logits[:], parts[:, :, 1], logits[:], ALU.add).then_inc(router_read, 1)
                    dve.wait_ge(router_read, b + 1)
                    for t in range(T):
                        ins = nc.vector.max(top_v[:, t], logits[:, t])
                    chain(ins)
                    if b > 0:
                        dve.wait_ge(gap_exp_ready, b)
                    nc.vector.tensor_tensor(gap[:], top_v[:, :, 1], top_v[:, :, 0], ALU.subtract)\
                        .then_inc(gap_ready, 1)
                    for t in range(T):
                        ins = nc.vector.max_index(top_i[:, t], top_v[:, t], logits[:, t])
                    chain(ins)
                    chain(nc.vector.tensor_copy(top_f[:], top_i[:, :, 0:2]))
                    chain(nc.vector.tensor_tensor(
                        picked[:], iota.unsqueeze(1).to_broadcast([P, 2 * T, E])
                        .rearrange("p (t a) e -> p t a e", a=2),
                        top_f[:].unsqueeze(3).to_broadcast([P, T, 2, E]), ALU.is_equal))
                    dve.wait_ge(gap_exp_ready, b + 1)
                    chain(nc.vector.tensor_scalar(gap_sum[:], gap_exp[:], 1.0, None, ALU.add))
                    chain(nc.vector.reciprocal(top_w[:, :, 0], gap_sum[:]))
                    chain(nc.vector.tensor_tensor(top_w[:, :, 1], gap_exp[:], top_w[:, :, 0], ALU.mult))
                    chain(nc.vector.tensor_tensor(picked[:], picked[:],
                                                  top_w[:].unsqueeze(3).to_broadcast([P, T, 2, E]), ALU.mult))
                    chain(nc.vector.tensor_tensor(combine[:], picked[:, :, 0], picked[:, :, 1], ALU.add))
                    if b > 0:
                        kc, nn = misc_of("comb", b - 1)
                        dve.wait_ge(misc_ready[kc], nn)
                    chain(nc.vector.tensor_copy(comb_st[:, :, 0:E], combine[:]))
                    nc.vector.tensor_tensor(comb_st[:, :, QUAD:QUAD + E], combine[:],
                                            comb_st[:, :, 0:E].bitcast(F32), ALU.subtract).then_inc(comb_st_ready, 1)

            def store(n):
                dve.wait_ge(down_done, (n + 1) * NU)
                if n >= 2:
                    dve.wait_ge(out_done[n % 2], 16 * (n // 2))
                nc.vector.tensor_tensor(y_sb[:, n % 2].rearrange("p t d -> p (t d)"), acc_ps[n % 2][:],
                                        x2[:, n].rearrange("p t d -> p (t d)"), ALU.add).then_inc(y_ready, 1)

            for n in range(B):
                for p in range(NU):
                    u = n * NU + p
                    c = n * NP + p
                    dve.wait_ge(silu_done, u + 1)
                    dve.wait_ge(up_ready, u + 1)
                    if p < NP:
                        nc.vector.tensor_tensor(hid_u[:, u % 2], up_ps[u % 2][:], silu[:, u % 2], ALU.mult)\
                            .then_inc(hid_u_done, 1)
                        dve.wait_ge(hid_u_done, c + 1)
                        dve.wait_ge(comb_ready, c + 1)
                        if u >= 3:
                            dve.wait_ge(down_done, u - 2)
                        nc.vector.tensor_tensor(hid[:, u % 3], comb_ps[u % 2][:], hid_u[:, u % 2], ALU.mult)\
                            .then_inc(hid_ready, 1)
                    else:
                        if u >= 3:
                            dve.wait_ge(down_done, u - 2)
                        nc.vector.tensor_tensor(hid[:, u % 3], up_ps[u % 2][:], silu[:, u % 2], ALU.mult)\
                            .then_inc(hid_ready, 1)
                    if p == 2 and n > 0:
                        store(n - 1)
            store(B - 1)

        @block.tensor
        def _(pe):
            def take(*use):
                k, n = misc_of(*use)
                if n > 1:
                    pe.wait_ge(*released(*uses[turn[use] - 2]))
                return misc[k], misc_ready[k]

            def transposes(use, src):
                ps, ready = take(*use)
                for t in range(T):
                    ins = nc.tensor.transpose(ps[:, t * P:(t + 1) * P], src(t), ident)
                ins.then_inc(ready, 1)

            pe.wait_ge(ld["ctx"], 16)
            pe.wait_ge(ld["wk"], 16)
            for g in range(G):
                ps, ready = take("k", g)
                nc.tensor.matmul(ps[:, 0:B * SK], wk_sb[:, g], ctx_sb[:].rearrange("c b k -> c (b k)"),
                                 start=True, stop=True).then_inc(ready, 1)
            pe.wait_ge(ctx_rep_ready, 1)
            pe.wait_ge(ld["wv"], 16)
            for b in range(B):
                ps, ready = take("v", b)
                for j, (a, z) in enumerate(KC):
                    ins = nc.tensor.matmul(ps[0:z - a, j * D:(j + 1) * D],
                                           ctx_rep[:, b].rearrange("c h k -> c (h k)")[:, a:z], wv_sb[:],
                                           start=True, stop=True)
                ins.then_inc(ready, 1)
            pe.wait_ge(ld["consts"], 16)

            def scores(i, m):
                t, g = m // G, m % G
                w = i * T * G + m
                if t == 0:
                    pe.wait_ge(q_lo_ready, i * G + g + 1)
                    pe.wait_ge(k_bd_ready, i * G + g + 1)
                if w >= 2:
                    pe.wait_ge(max_done, w - 1)
                nc.tensor.matmul(sq_ps[w % 2][:, 0:GK], q_st[:, i % 2, g, t * P:(t + 1) * P], k_bd[:, g, i],
                                 start=True, stop=True).then_inc(sq_ready, 1)

            def scores_t(b, m):
                j, g = m // G, m % G
                e = b * NJ * G + m
                a, z = KC[j]
                if j == 0:
                    pe.wait_ge(q_max_ready, b * G + g + 1)
                if e >= 2:
                    pe.wait_ge(exp_done, e - 1)
                nc.tensor.matmul(st_ps[e % 2][0:z - a, :], k_bd[:, g, b, a:z], q_st[:, b % 2, g],
                                 start=True, stop=True).then_inc(st_ready, 1)

            def weigh(b, j):
                a, z = KC[j]
                if j == 0:
                    pe.wait_ge(v_bd_ready, b + 1)
                    if b > 0:
                        pe.wait_ge(den_copied, b)
                        pe.wait_ge(att_ready, b)
                for out_ps, lhs in ((po, v_bd[0:z - a, b, j]), (pd, v_mask[0:z - a, j])):
                    for g in range(G):
                        e = b * NJ * G + j * G + g
                        pe.wait_ge(exp_done, e + 1)
                        q = slice(QUAD * g, QUAD * (g + 1))
                        ins = nc.tensor.matmul(out_ps[q, :], lhs[:, q], probs[0:z - a, e % 8],
                                               start=(j == 0), stop=(j == NJ - 1))
                ins.then_inc(pv_done, 1)

            for i in range(B + 3):
                b = i - 2
                if 0 <= i - 3 < B:
                    pe.wait_ge(comb_st_ready, i - 2)
                    transposes(("comb", i - 3), lambda t: comb_st[:, t].bitcast(F32))
                if 0 <= b < B:
                    pe.wait_ge(den_copied, b + 1)
                    transposes(("den", b), lambda t: den_sb[:, t * P:(t + 1) * P])
                if i < B:
                    pe.wait_ge(xn_ready[0], i + 1)
                    transposes(("xt", i), lambda t: xn[:, 0, t])
                    if i == 0:
                        pe.wait_ge(wq_split, 1)
                    pe.wait_ge(xt_hi_ready, i + 1)
                    pe.wait_ge(xt_lo_ready, i + 1)
                    for g in range(G):
                        ps, ready = take("q", i, g)
                        nc.tensor.matmul(ps[:, 0:S], wq_hi[:, g], xt_hi[:], start=True, stop=False)
                        nc.tensor.matmul(ps[:, 0:S], wq_lo[:, g], xt_hi[:], start=False, stop=False)
                        nc.tensor.matmul(ps[:, 0:S], wq_hi[:, g], xt_lo[:], start=False, stop=True)\
                            .then_inc(ready, 1)
                if 0 <= b < B:
                    pe.wait_ge(den_rep_ready, b + 1)
                    transposes(("inv", b), lambda t: den_rep[:, t])
                for m in range(T * G):
                    if i < B:
                        scores(i, m)
                    if 0 <= i - 1 < B and m < NJ * G:
                        scores_t(i - 1, m)
                    if 0 <= i - 1 < B and m in (6, 10, 14):
                        weigh(i - 1, (m - 6) // G)
                    if m == 7 and 0 <= b < B:
                        ps, ready = take("wo", b)
                        if b == 0:
                            pe.wait_ge(ld["wo"], 16)
                        pe.wait_ge(att_ready, b + 1)
                        for t in range(T):
                            ins = nc.tensor.matmul(ps[:, t * D:(t + 1) * D], att_t[:, t * P:(t + 1) * P], wo_sb[:],
                                                   start=True, stop=True)
                        ins.then_inc(ready, 1)
                if 0 <= b < B:
                    pe.wait_ge(xn_ready[1], b + 1)
                    transposes(("x2t", b), lambda t: xn[:, 1, t])
                if i < B:
                    pe.wait_ge(max_st_ready, i + 1)
                    transposes(("max", i), lambda t: max_st[:, t].bitcast(F32))
                if 0 <= b < B:
                    ps, ready = take("router", b)
                    if b == 0:
                        pe.wait_ge(rw_split, 1)
                    pe.wait_ge(x2t_hi_ready, b + 1)
                    pe.wait_ge(x2t_lo_ready, b + 1)
                    for t in range(T):
                        tok = slice(b * S + t * P, b * S + (t + 1) * P)
                        nc.tensor.matmul(ps[:, t * 2 * E:t * 2 * E + E], x2t_lo[:, tok], rw_st[:, 0],
                                         start=True, stop=False, skip_group_check=True)
                        ins = nc.tensor.matmul(ps[:, t * 2 * E:(t + 1) * 2 * E], x2t_hi[:, tok],
                                               rw_st[:].rearrange("p a e -> p (a e)"), start=False, stop=True,
                                               skip_group_check=True)
                    ins.then_inc(ready, 1)

            pe.wait_ge(comb_t_ready, B)
            pe.wait_ge(att_ready, B)
            pe.wait_ge(den_copied, B)
            pe.wait_ge(max_done, B * T * G)
            pe.wait_ge(w_lo_ready, 2)
            pe.wait_ge(sel_ready, 1)
            pe.wait_ge(ld["wd"], 32)

            def down_proj(n, p):
                u = n * NU + p
                acc = acc_ps[n % 2]
                pe.wait_ge(hid_ready, u + 1)
                if p == 0 and n >= 2:
                    pe.wait_ge(y_ready, n - 1)
                for t in range(T):
                    ins = nc.tensor.matmul(acc[:, t * D:(t + 1) * D], hid[:, u % 3, t * P:(t + 1) * P],
                                           wd_sb[:, p], start=(p == 0 and t == 0), stop=(p == NU - 1),
                                           skip_group_check=True)
                ins.then_inc(down_done, 1)

            for n in range(B):
                tok = slice(n * S, (n + 1) * S)
                for p in range(NU):
                    u = n * NU + p
                    for ps, hi, lo, ready, free in ((gate_ps, wg_hi, wg_lo, gate_ready, gate_read),
                                                    (up_ps, wu_hi, wu_lo, up_ready, up_read)):
                        if u >= 2:
                            pe.wait_ge(*free(u - 2))
                        nc.tensor.matmul(ps[u % 2][:], hi[:, p], x2t_hi[:, tok], start=True, stop=False)
                        nc.tensor.matmul(ps[u % 2][:], hi[:, p], x2t_lo[:, tok], start=False, stop=False)
                        nc.tensor.matmul(ps[u % 2][:], lo[:, p], x2t_hi[:, tok], start=False, stop=True)\
                            .then_inc(ready, 1)
                    if p < NP:
                        if u >= 2:
                            pe.wait_ge(hid_ready, u - 1)
                        nc.tensor.matmul(comb_ps[u % 2][:], sel[:, 2 * p:2 * p + 2].rearrange("p e f -> p (e f)"),
                                         comb_t[:, tok], start=True, stop=True).then_inc(comb_ready, 1)
                    if u >= 1:
                        down_proj((u - 1) // NU, (u - 1) % NU)
            down_proj(B - 1, NU - 1)


_ARGS = ["x", "ctx_t", "wq", "bq", "wk", "wv", "wo", "bo", "router_t", "router_bias", "up", "gate", "down",
         "sh_gate_t", "sh_up_t", "sh_down_t", "consts"]


def kernel(**inputs):
    import numpy as np
    from concourse import bacc
    from concourse.bass_utils import run_bass_kernel_spmd

    a = {n.replace("L0_xattn_", "").replace("L0_ffn_", ""): np.asarray(v) for n, v in inputs.items()}
    x, y = a["x"], a["ctx_768"]
    B, SK, C = y.shape
    D = x.shape[2]
    E = a["up_proj"].shape[0]
    QUAD, G, HG, P = 32, 4, 4, 128
    HD = D // (G * HG)
    chunks = [(0, 104), (104, 206), (206, 308)]

    ctx_t = np.ones((C + 1, B, SK), x.dtype)
    ctx_t[:C] = y.transpose(2, 0, 1)
    wq = np.zeros((D, G, P), x.dtype)
    bq = np.zeros((P, G), x.dtype)
    wk = np.zeros((C + 1, G, P), x.dtype)
    for g in range(G):
        cols = slice(QUAD * g, QUAD * (g + 1))
        for a4 in range(4):
            here = slice(QUAD * a4, QUAD * (a4 + 1))
            if a4 != g:
                wq[:, g, here] = a["wq"][:, cols]
                bq[here, g] = a["bq"][cols]
                wk[:C, g, here] = a["wk"][:, cols]
                wk[C, g, here] = a["bk"][cols]
            else:
                wk[C, g, here] = 1.0
    wv = np.concatenate([a["wv"], a["bv"][None]], 0)

    row = np.arange(P)
    k_mask = np.zeros((P, G, HG), x.dtype)
    for g in range(G):
        for h in range(HG):
            k_mask[:, g, h] = (row % QUAD) // HD == h
            own = row // QUAD == g
            k_mask[own, g, h] = ((row % QUAD) % HG == h)[own] & ((row % QUAD) < 2 * HG)[own]
    v_mask = np.zeros((P, len(chunks), D), x.dtype)
    for j, (lo, hi) in enumerate(chunks):
        for r in range(hi - lo):
            v_mask[r, j] = (np.arange(D) % QUAD) // HD == (lo + r) // SK
    pair_rows = np.zeros((P, E), x.dtype)
    for e in range(E):
        pair_rows[e, e] = pair_rows[QUAD + e, e] = 1.0
    iota = np.tile(np.arange(E, dtype=x.dtype), (P, 1))
    consts = np.concatenate([np.eye(P, dtype=x.dtype), k_mask.reshape(P, -1), v_mask.reshape(P, -1), pair_rows,
                             iota], 1)

    laid = {
        "x": x, "ctx_t": ctx_t, "wq": wq, "bq": bq, "wk": wk, "wv": wv, "wo": a["wo"], "bo": a["bo"],
        "router_t": a["router_w"].T, "router_bias": a["router_bias"], "up": a["up_proj"], "gate": a["gate_proj"],
        "down": a["down_proj"], "sh_gate_t": a["sh_gate"].T, "sh_up_t": a["sh_up"].T, "sh_down_t": a["sh_down"].T,
        "consts": consts,
    }
    nc = bacc.Bacc("TRN2", target_bir_lowering=False, num_devices=1)
    arrays, aps = {}, []
    for name in _ARGS:
        arr = np.ascontiguousarray(laid[name])
        arrays[f"in_{name}"] = arr
        aps.append(nc.dram_tensor(f"in_{name}", arr.shape, mybir.dt.from_np(arr.dtype), kind="ExternalInput").ap())
    aps.append(nc.dram_tensor("out_y", x.shape, F32, kind="ExternalOutput").ap())
    build(nc, *aps)
    r = run_bass_kernel_spmd(nc, [arrays], core_ids=[0])
    return r.results[0]["out_y"]
```

```python
from contextlib import ExitStack

import concourse.bass as bass
from concourse import mybir

F32 = mybir.dt.float32
F32R = mybir.dt.float32r
U32 = mybir.dt.uint32
ALU = mybir.AluOpType
ACT = mybir.ActivationFunctionType
AX = mybir.AxisListType

P = 128
QUAD = 32
EPS = 1e-5


def build(nc, x, ctx_t, wq, bq, wk, wv, wo, bo, router_t, router_bias, up, gate, down,
          sh_gate_t, sh_up_t, sh_down_t, consts, v_mask_c, out):
    B, S, D = x.shape
    H, HD = 16, D // 16
    G, HG = 4, 4
    SK = ctx_t.shape[2]
    C1 = ctx_t.shape[0]
    GK = HG * SK
    KC = [(0, 104), (104, 206), (206, 308)]
    NJ = len(KC)
    T = S // P
    E, _, F = up.shape
    NP = E // 2
    NU = NP + 1
    SCALE = float(HD) ** -0.5
    assert D == P and GK == KC[-1][1] and 2 * F == P and HG * HD == QUAD

    ctx = ExitStack()
    with ctx:
        def sb(name, shape, dt=F32):
            return ctx.enter_context(nc.sbuf_tensor(name, shape, dt))

        def sem(name):
            return ctx.enter_context(nc.semaphore(name))

        x_sb = sb("x_sb", [P, B, T, D])
        x_bo = sb("x_bo", [P, B, T, D])
        x2 = sb("x2", [P, B, T, D])
        ctx_sb = sb("ctx_sb", [C1, B, SK])
        ctx_rep = sb("ctx_rep", [C1, B, HG, SK])
        cst = sb("cst", [P, consts.shape[1]])
        ident = cst[:, 0:P]
        k_mask = cst[:, P:P + G * HG].rearrange("p (g h) -> p g h", g=G)
        pair_rows = cst[:, P + G * HG:P + G * HG + E]
        iota = cst[:, P + G * HG + E:P + G * HG + 2 * E]
        v_mask = sb("v_mask", [P, NJ, D])
        wq_sb = sb("wq_sb", [P, G, P])
        wq_hi = sb("wq_hi", [P, G, P], F32R)
        wq_lo = sb("wq_lo", [P, G, P], F32R)
        bq_sb = sb("bq_sb", [P, G])
        wk_sb = sb("wk_sb", [C1, G, P])
        wv_sb = sb("wv_sb", [C1, D])
        wo_sb = sb("wo_sb", [P, D])
        bo_sb = sb("bo_sb", [P, D])
        rw_sb = sb("rw_sb", [P, E])
        rw_st = sb("rw_st", [P, 2, E], F32R)
        rb_sb = sb("rb_sb", [P, E])
        wg_sb = sb("wg_sb", [P, NU, P])
        wu_sb = sb("wu_sb", [P, NU, P])
        wg_hi = sb("wg_hi", [P, NU, P], F32R)
        wg_lo = sb("wg_lo", [P, NU, P], F32R)
        wu_hi = sb("wu_hi", [P, NU, P], F32R)
        wu_lo = sb("wu_lo", [P, NU, P], F32R)
        wd_sb = sb("wd_sb", [P, NU, D])
        sel = sb("sel", [P, E, F], F32R)

        k_st = sb("k_st", [P, G, B * SK], F32R)
        k_bd = sb("k_bd", [P, G, B, GK], F32R)
        v_bd = sb("v_bd", [P, B, NJ, D])
        stats = sb("stats", [P, 2, T, 6])
        mean_var = sb("mean_var", [P, 2, T, 2])
        var_eps = sb("var_eps", [P, 2, T])
        rstd = sb("rstd", [P, 2, T])
        minus_half = sb("minus_half", [P, T])
        xn = sb("xn", [P, 2, T, D])
        xt_hi = sb("xt_hi", [P, S], F32R)
        xt_lo = sb("xt_lo", [P, S], F32R)
        q_st = sb("q_st", [P, 2, G, S], F32R)
        neg_max = sb("neg_max", [P, T, H])
        max_st = sb("max_st", [P, T, P], F32R)
        probs = sb("probs", [P, 8, S])
        den_sb = sb("den_sb", [P, S])
        den_inv = sb("den_inv", [P, T, H])
        den_rep = sb("den_rep", [P, T, D])
        inv_t = sb("inv_t", [P, S])
        att_t = sb("att_t", [P, S])
        x2t_hi = sb("x2t_hi", [P, B * S], F32R)
        x2t_lo = sb("x2t_lo", [P, B * S], F32R)
        logits = sb("logits", [P, T, E])
        top_v = sb("top_v", [P, T, 8])
        top_i = sb("top_i", [P, T, 8], U32)
        top_f = sb("top_f", [P, T, 2])
        gap = sb("gap", [P, T])
        gap_exp = sb("gap_exp", [P, T])
        gap_sum = sb("gap_sum", [P, T])
        top_w = sb("top_w", [P, T, 2])
        picked = sb("picked", [P, T, 2, E])
        combine = sb("combine", [P, T, E])
        comb_st = sb("comb_st", [P, T, P], F32R)
        comb_t = sb("comb_t", [P, B * S], F32R)
        silu = sb("silu", [P, 2, S])
        hid_u = sb("hid_u", [P, 2, S])
        hid = sb("hid", [P, 3, S])
        y_sb = sb("y_sb", [P, 2, T, D])

        banks = [ctx.enter_context(nc.psum_tensor(f"bank{i}", [P, 512], F32)) for i in range(8)]
        misc = [*banks[0:2], *banks[4:6]]
        sq_ps = banks[2:4]
        st_ps = banks[4:6]
        po, pd = banks[6], banks[7]
        gate_ps, up_ps, acc = sq_ps, st_ps, pd

        names = ("consts", "v_mask", "ctx", "wk", "wv", "wq", "bq", "wo", "bo", "rw", "rb", "wgu", "wd")
        ld = {n: sem(f"ld_{n}") for n in names}
        ld_x = [sem(f"ld_x{b}") for b in range(B)]
        misc_ready = [sem(f"misc{k}_ready") for k in range(4)]
        dve_step = sem("dve_step")
        var_ready = [sem("var1_ready"), sem("var2_ready")]
        rstd_ready = [sem("rstd1_ready"), sem("rstd2_ready")]
        picked_ready = sem("picked_ready")
        zeroed = sem("zeroed")
        ctx_rep_ready = sem("ctx_rep_ready")
        wq_split = sem("wq_split")
        rw_split = sem("rw_split")
        k_hi_ready = sem("k_hi_ready")
        k_st_ready = sem("k_st_ready")
        k_bd_ready = sem("k_bd_ready")
        v_bd_ready = sem("v_bd_ready")
        stats_ready = [sem("stats1_ready"), sem("stats2_ready")]
        xn_ready = [sem("xn1_ready"), sem("xn2_ready")]
        x_bo_ready = sem("x_bo_ready")
        xt_hi_ready = sem("xt_hi_ready")
        xt_lo_ready = sem("xt_lo_ready")
        q_hi_ready = sem("q_hi_ready")
        q_lo_ready = sem("q_lo_ready")
        sq_ready = sem("sq_ready")
        max_done = sem("max_done")
        max_st_ready = sem("max_st_ready")
        q_max_ready = sem("q_max_ready")
        st_ready = sem("st_ready")
        exp_done = sem("exp_done")
        pv_done = sem("pv_done")
        den_copied = sem("den_copied")
        den_inv_ready = sem("den_inv_ready")
        den_rep_ready = sem("den_rep_ready")
        inv_t_ready = sem("inv_t_ready")
        att_ready = sem("att_ready")
        x2_ready = sem("x2_ready")
        x2t_hi_ready = sem("x2t_hi_ready")
        x2t_lo_ready = sem("x2t_lo_ready")
        router_read = sem("router_read")
        gap_ready = sem("gap_ready")
        gap_exp_ready = sem("gap_exp_ready")
        comb_st_ready = sem("comb_st_ready")
        comb_t_ready = sem("comb_t_ready")
        w_hi_ready = sem("w_hi_ready")
        w_lo_ready = sem("w_lo_ready")
        sel_ready = sem("sel_ready")
        gate_ready = sem("gate_ready")
        up_ready = sem("up_ready")
        silu_done = sem("silu_done")
        hid_u_done = sem("hid_u_done")
        hid_ready = sem("hid_ready")
        down_done = sem("down_done")
        y_ready = sem("y_ready")
        out_done = [sem("out_done_even"), sem("out_done_odd")]

        def plan(i):
            head, tail, full = i < B, 0 <= i - 2 < B, i >= 3
            turns = {m: [] for m in range(T * G + 1)}
            if head:
                slots = [[("xt", 0)], [("den", 0), ("q", 0)], [("max", 0), ("q", 1)], [("inv", 0), ("q", 2)],
                         [("wo", 0), ("q", 3)], [("moments", 0), ("split_router", 0)], [], [], []]
                if full:
                    slots[6] += [("norm", 0)]
                    slots[7] += [("x2t", 0)]
                else:
                    slots[7] += [("v", b) for b in range(B)]
                    turns[3] += [("norm", 0)]
                    turns[6] += [("x2t", 0)]
                turns[2 if full else 9] += [("router", 0)]
                turns[3] += [("norm_next", 0)]
                turns[6 if full else 12] += [("route", 0)]
                turns[9 if full else 15] += [("gap_exp", 0)]
                turns[10 if full else 16] += [("combine", 0)]
                turns[16] += [("place_max", 0)]
            else:
                slots = [[("den", 0), ("max", 0)], [("inv", 0)], [("wo", 0)], [], [("norm", 0)], [("x2t", 0)],
                         [("router", 0)], [("route", 0)], [("gap_exp", 0), ("combine", 0)]]
            turns[1] += [("store", 0)]
            turns[16] += [("comb", 0)]
            return slots, turns

        def active(i, kind):
            if kind in ("xt", "q", "place_max"):
                return i < B
            if kind in ("moments", "norm_next"):
                return i + 1 < B
            if kind == "split_router":
                return i == 0
            if kind == "v":
                return i == 1
            if kind == "max":
                return 0 <= i - 1 < B
            if kind == "store":
                return 0 <= i - 3 < B
            return 0 <= i - 2 < B

        PLAN = []
        for i in range(B + 3):
            slots, turns = plan(i)
            PLAN.append(([[st for st in here if active(i, st[0])] for here in slots],
                         {m: [st for st in here if active(i, st[0])] for m, here in turns.items()}))

        BATCH = {"xt": 0, "q": 0, "max": 1, "den": 2, "inv": 2, "wo": 2, "x2t": 2, "router": 2, "comb": 2}

        def use_of(i, kind, g):
            return ("v", g, 0) if kind == "v" else (kind, i - BATCH[kind], g)

        uses, bank_of, count_of, before = [], {}, {}, {}
        last_on = [None] * 4
        filled = [0] * 4
        st_last = {}
        st_first = set()

        def use_bank(use, k):
            before[use] = last_on[k]
            last_on[k] = use
            filled[k] += 1
            bank_of[use], count_of[use] = k, filled[k]
            uses.append(use)

        for g in range(G):
            use_bank(("k", g, 0), g)
        turn = 0
        for i, (slots, turns) in enumerate(PLAN):
            width = 4 if i < 3 else 2
            fresh = {2, 3}
            for p, here in enumerate(slots):
                if i >= 3 and p < NP:
                    use_bank(("spread", i - 3, p), turn % 2)
                    turn += 1
                for kind, g in here:
                    if kind in BATCH or kind == "v":
                        k = turn % width
                        use_bank(use_of(i, kind, g), k)
                        if k in fresh:
                            st_first.add(use_of(i, kind, g))
                            fresh.discard(k)
                        turn += 1
            st_last[i] = [last_on[2], last_on[3]]
            for m in range(T * G + 1):
                for kind, g in turns[m]:
                    if kind in BATCH:
                        use_bank(use_of(i, kind, g), turn % 2)
                        turn += 1

        def misc_of(*use):
            return bank_of[use], count_of[use]

        def released(kind, i, g=0):
            return {"k": (k_st_ready, i + 1), "v": (v_bd_ready, i + 1), "comb": (comb_t_ready, i + 1),
                    "den": (den_inv_ready, i + 1), "xt": (xt_lo_ready, i + 1), "q": (q_lo_ready, i * G + g + 1),
                    "inv": (inv_t_ready, i + 1), "wo": (x2_ready, i + 1), "x2t": (x2t_lo_ready, i + 1),
                    "max": (q_max_ready, (i + 1) * G), "router": (router_read, i + 1),
                    "spread": (hid_ready, i * NU + g + 1)}[kind]

        def gate_read(u):
            return silu_done, u + 1

        def up_read(u):
            n, p = u // NU, u % NU
            return (hid_u_done, n * NP + p + 1) if p < NP else (hid_ready, u + 1)

        def quads(g):
            return [a for a in range(4) if a != g]

        block = ctx.enter_context(nc.Block())

        @block.sync
        def _(sp):
            sp.dma_start(x_sb[:, 0], x[0].rearrange("(t p) d -> p t d", p=P)).then_inc(ld_x[0], 16)
            sp.dma_start(wq_sb[:], wq).then_inc(ld["wq"], 16)
            sp.dma_start(cst[:], consts).then_inc(ld["consts"], 16)
            sp.dma_start(bq_sb[:], bq).then_inc(ld["bq"], 16)
            sp.dma_start(wv_sb[:], wv).then_inc(ld["wv"], 16)
            sp.dma_start(v_mask[:], v_mask_c).then_inc(ld["v_mask"], 16)
            for b in range(1, B):
                sp.dma_start(x_sb[:, b], x[b].rearrange("(t p) d -> p t d", p=P)).then_inc(ld_x[b], 16)
            sp.dma_start(bo_sb[:], bo.partition_broadcast(P)).then_inc(ld["bo"], 16)
            sp.dma_start(wo_sb[:], wo).then_inc(ld["wo"], 16)
            sp.dma_start(rw_sb[:], router_t).then_inc(ld["rw"], 16)
            sp.dma_start(rb_sb[:], router_bias.partition_broadcast(P)).then_inc(ld["rb"], 16)
            sp.dma_start(wg_sb[:, 0:NP, :].rearrange("p n (a f) -> p (n a) f", a=2),
                         gate.rearrange("e d f -> d e f")).then_inc(ld["wgu"], 16)
            sp.dma_start(wg_sb[:, NP, :], sh_gate_t).then_inc(ld["wgu"], 16)
            sp.dma_start(wu_sb[:, 0:NP, :].rearrange("p n (a f) -> p (n a) f", a=2),
                         up.rearrange("e d f -> d e f")).then_inc(ld["wgu"], 16)
            sp.dma_start(wu_sb[:, NP, :], sh_up_t).then_inc(ld["wgu"], 16)
            sp.dma_start(wd_sb[:, 0:NP, :], down.rearrange("(n a) f d -> (a f) n d", a=2)).then_inc(ld["wd"], 16)
            sp.dma_start(wd_sb[:, NP, :], sh_down_t).then_inc(ld["wd"], 16)
            for n in range(B):
                sp.wait_ge(y_ready, n + 1)
                sp.dma_start(out[n].rearrange("(t p) d -> p t d", p=P), y_sb[:, n % 2])\
                    .then_inc(out_done[n % 2], 16)
            sp.wait_ge(out_done[0], 16 * (B // 2))
            sp.wait_ge(out_done[1], 16 * (B // 2))

        @block.gpsimd
        def _(pool):
            def inverse_root(which, n):
                pool.wait_ge(stats_ready[which], n + 1)
                nc.gpsimd.tensor_scalar(var_eps[:, which], mean_var[:, which, :, 1], EPS, None, ALU.add)\
                    .then_inc(var_ready[which], 1)
                pool.wait_ge(var_ready[which], n + 1)
                nc.gpsimd.tensor_tensor(rstd[:, which], var_eps[:, which], minus_half[:], ALU.pow)\
                    .then_inc(rstd_ready[which], 1)

            def expand_k(b):
                for g in range(G):
                    if b == 0:
                        pool.wait_ge(k_st_ready, g + 1)
                    keys = k_st[:, g, b * SK:(b + 1) * SK].bitcast(F32)
                    nc.gpsimd.tensor_tensor(
                        k_bd[:, g, b].rearrange("p (h k) -> p h k", h=HG),
                        keys.unsqueeze(1).to_broadcast([P, HG, SK]),
                        k_mask[:, g].unsqueeze(2).to_broadcast([P, HG, SK]), ALU.mult).then_inc(k_bd_ready, 1)

            def add_bo(b):
                pool.wait_ge(ld_x[b], 16)
                nc.gpsimd.tensor_tensor(x_bo[:, b], x_sb[:, b], bo_sb[:].unsqueeze(1).to_broadcast([P, T, D]),
                                        ALU.add).then_inc(x_bo_ready, 1)

            nc.gpsimd.memset(minus_half[:], -0.5).then_inc(zeroed, 1)
            nc.gpsimd.memset(max_st[:].bitcast(F32), 0.0).then_inc(zeroed, 1)
            nc.gpsimd.memset(comb_st[:].bitcast(F32), 0.0).then_inc(zeroed, 1)
            pool.wait_ge(zeroed, 3)
            inverse_root(0, 0)
            pool.wait_ge(ld["consts"], 16)
            expand_k(0)
            inverse_root(0, 1)
            expand_k(1)
            pool.wait_ge(ld["bo"], 16)
            add_bo(0)
            nc.gpsimd.tensor_copy(sel[:], pair_rows.unsqueeze(2).to_broadcast([P, E, F])).then_inc(sel_ready, 1)
            expand_k(2)
            inverse_root(0, 2)
            add_bo(1)
            pool.wait_ge(w_hi_ready, 1)
            nc.gpsimd.tensor_tensor(wg_lo[:], wg_sb[:], wg_hi[:].bitcast(F32), ALU.subtract).then_inc(w_lo_ready, 1)
            inverse_root(1, 0)
            expand_k(3)
            add_bo(2)
            inverse_root(0, 3)
            pool.wait_ge(w_hi_ready, 2)
            nc.gpsimd.tensor_tensor(wu_lo[:], wu_sb[:], wu_hi[:].bitcast(F32), ALU.subtract).then_inc(w_lo_ready, 1)
            add_bo(3)
            for b in range(1, B):
                inverse_root(1, b)

        @block.scalar
        def _(act):
            def copy_misc(dst, *use, done):
                k, n = misc_of(*use)
                act.wait_ge(misc_ready[k], n)
                nc.scalar.activation(dst, misc[k][:, 0:dst.shape[-1]], ACT.Copy).then_inc(done, 1)

            def expert(n, p):
                u = n * NU + p
                act.wait_ge(gate_ready, u + 1)
                if u >= 2:
                    act.wait_ge(*up_read(u - 2))
                nc.scalar.activation(silu[:, u % 2], gate_ps[p % 2][:], ACT.Silu).then_inc(silu_done, 1)

            def side_step(i, kind, g):
                if kind == "max":
                    k, n = misc_of("max", i - 1, 0)
                    act.wait_ge(misc_ready[k], n)
                    for g in range(G):
                        a = slice(QUAD * g, QUAD * (g + 1))
                        nc.scalar.activation(q_st[a, (i - 1) % 2, g], misc[k][a, 0:S], ACT.Copy)\
                            .then_inc(q_max_ready, 1)
                elif kind == "xt":
                    copy_misc(xt_hi[:], "xt", i, 0, done=xt_hi_ready)
                elif kind == "q":
                    k, n = misc_of("q", i, g)
                    act.wait_ge(misc_ready[k], n)
                    if i == 0:
                        act.wait_ge(ld["bq"], 16)
                    nc.scalar.activation(q_st[:, i % 2, g], misc[k][:, 0:S], ACT.Identity,
                                         bias=bq_sb[:, g:g + 1]).then_inc(q_hi_ready, 1)
                elif kind == "inv":
                    copy_misc(inv_t[:], "inv", i - 2, 0, done=inv_t_ready)
                elif kind == "x2t":
                    copy_misc(x2t_hi[:, (i - 2) * S:(i - 1) * S], "x2t", i - 2, 0, done=x2t_hi_ready)
                elif kind == "gap_exp":
                    act.wait_ge(gap_ready, i - 1)
                    nc.scalar.activation(gap_exp[:], gap[:], ACT.Exp).then_inc(gap_exp_ready, 1)
                elif kind == "comb":
                    copy_misc(comb_t[:, (i - 2) * S:(i - 1) * S], "comb", i - 2, 0, done=comb_t_ready)

            def probabilities(b, m):
                e = b * NJ * G + m
                rows = KC[m // G][1] - KC[m // G][0]
                act.wait_ge(st_ready, e + 1)
                if e >= 8:
                    act.wait_ge(pv_done, (e - 8) // G + 1)
                nc.scalar.activation(probs[0:rows, e % 8], st_ps[e % 2][0:rows, :], ACT.Exp,
                                     scale=SCALE).then_inc(exp_done, 1)

            act.dma_start(ctx_sb[:], ctx_t).then_inc(ld["ctx"], 16)
            act.dma_start(wk_sb[:], wk).then_inc(ld["wk"], 16)
            for g in range(G):
                copy_misc(k_st[:, g], "k", g, 0, done=k_hi_ready)
            for i, (slots, turns) in enumerate(PLAN):
                for p, here in enumerate(slots):
                    if i >= 3:
                        expert(i - 3, p)
                    for kind, g in here:
                        side_step(i, kind, g)
                if i == 0:
                    for b in range(B):
                        nc.scalar.activation(ctx_rep[:, b], ctx_sb[:, b].unsqueeze(1).to_broadcast([C1, HG, SK]),
                                             ACT.Copy).then_inc(ctx_rep_ready, 1)
                for m in range(T * G + 1):
                    if 0 <= i - 1 < B and m < NJ * G:
                        probabilities(i - 1, m)
                    if m == T * G and 0 <= i - 1 < B:
                        act.wait_ge(pv_done, NJ * i)
                        if i >= 2:
                            k, n = misc_of("den", i - 2, 0)
                            act.wait_ge(misc_ready[k], n)
                        nc.scalar.activation(den_sb[:], pd[:], ACT.Copy).then_inc(den_copied, 1)
                    for kind, g in turns[m]:
                        side_step(i, kind, g)
                if i == 1:
                    act.wait_ge(ld["wgu"], 64)
                    nc.scalar.activation(wg_hi[:], wg_sb[:], ACT.Copy).then_inc(w_hi_ready, 1)
                    nc.scalar.activation(wu_hi[:], wu_sb[:], ACT.Copy).then_inc(w_hi_ready, 1)

        @block.vector
        def _(dve):
            steps = [0]

            def chain(ins):
                ins.then_inc(dve_step, 1)
                steps[0] += 1
                dve.wait_ge(dve_step, steps[0])

            def moments(which, n, src):
                for t in range(T):
                    ins = nc.vector.bn_stats(stats[:, which, t], src[:, n, t])
                chain(ins)
                for t in range(T):
                    ins = nc.vector.bn_aggr(mean_var[:, which, t], stats[:, which, t])
                ins.then_inc(stats_ready[which], 1)

            def normalise(which, n, src):
                dve.wait_ge(rstd_ready[which], n + 1)
                if n > 0:
                    k, turns = misc_of(("xt", "x2t")[which], n - 1, 0)
                    dve.wait_ge(misc_ready[k], turns)
                for t in range(T):
                    ins = nc.vector.tensor_scalar(xn[:, which, t], src[:, n, t], mean_var[:, which, t, 0:1],
                                                  rstd[:, which, t:t + 1], ALU.subtract, ALU.mult)
                ins.then_inc(xn_ready[which], 1)

            def low_part(dst, hi, *use, hi_ready, done):
                k, n = misc_of(*use)
                dve.wait_ge(hi_ready, use[1] + 1)
                nc.vector.tensor_tensor(dst, misc[k][:, 0:S], hi.bitcast(F32), ALU.subtract).then_inc(done, 1)

            def expert(n, p):
                u = n * NU + p
                dve.wait_ge(silu_done, u + 1)
                dve.wait_ge(up_ready, u + 1)
                if p < NP:
                    nc.vector.tensor_tensor(hid_u[:, u % 2], up_ps[p % 2][:], silu[:, u % 2], ALU.mult)\
                        .then_inc(hid_u_done, 1)
                    dve.wait_ge(hid_u_done, n * NP + p + 1)
                    k, turns = misc_of("spread", n, p)
                    dve.wait_ge(misc_ready[k], turns)
                    if u >= 3:
                        dve.wait_ge(down_done, u - 2)
                    nc.vector.tensor_tensor(hid[:, u % 3], misc[k][:], hid_u[:, u % 2], ALU.mult)\
                        .then_inc(hid_ready, 1)
                else:
                    dve.wait_ge(down_done, u - 2)
                    nc.vector.tensor_tensor(hid[:, u % 3], up_ps[p % 2][:], silu[:, u % 2], ALU.mult)\
                        .then_inc(hid_ready, 1)

            def route(b):
                k, n = misc_of("router", b, 0)
                dve.wait_ge(misc_ready[k], n)
                if b == 0:
                    dve.wait_ge(ld["rb"], 16)
                parts = misc[k][:, 0:T * 2 * E].rearrange("p (t a e) -> p t a e", a=2, e=E)
                chain(nc.vector.tensor_tensor(logits[:], parts[:, :, 0], rb_sb[:].unsqueeze(1)
                                              .to_broadcast([P, T, E]), ALU.add))
                nc.vector.tensor_tensor(logits[:], parts[:, :, 1], logits[:], ALU.add).then_inc(router_read, 1)
                dve.wait_ge(router_read, b + 1)
                for t in range(T):
                    ins = nc.vector.max(top_v[:, t], logits[:, t])
                chain(ins)
                nc.vector.tensor_tensor(gap[:], top_v[:, :, 1], top_v[:, :, 0], ALU.subtract)\
                    .then_inc(gap_ready, 1)
                for t in range(T):
                    ins = nc.vector.max_index(top_i[:, t], top_v[:, t], logits[:, t])
                chain(ins)
                chain(nc.vector.tensor_copy(top_f[:], top_i[:, :, 0:2]))
                nc.vector.tensor_tensor(
                    picked[:], iota.unsqueeze(1).to_broadcast([P, 2 * T, E])
                    .rearrange("p (t a) e -> p t a e", a=2),
                    top_f[:].unsqueeze(3).to_broadcast([P, T, 2, E]), ALU.is_equal).then_inc(picked_ready, 1)

            def combine_weights(b):
                dve.wait_ge(gap_exp_ready, b + 1)
                chain(nc.vector.tensor_scalar(gap_sum[:], gap_exp[:], 1.0, None, ALU.add))
                chain(nc.vector.reciprocal(top_w[:, :, 0], gap_sum[:]))
                chain(nc.vector.tensor_tensor(top_w[:, :, 1], gap_exp[:], top_w[:, :, 0], ALU.mult))
                dve.wait_ge(picked_ready, b + 1)
                chain(nc.vector.tensor_tensor(picked[:], picked[:],
                                              top_w[:].unsqueeze(3).to_broadcast([P, T, 2, E]), ALU.mult))
                chain(nc.vector.tensor_tensor(combine[:], picked[:, :, 0], picked[:, :, 1], ALU.add))
                chain(nc.vector.tensor_copy(comb_st[:, :, 0:E], combine[:]))
                nc.vector.tensor_tensor(comb_st[:, :, QUAD:QUAD + E], combine[:],
                                        comb_st[:, :, 0:E].bitcast(F32), ALU.subtract).then_inc(comb_st_ready, 1)

            def row_maximum(i, m):
                t, g = m // G, m % G
                w = i * T * G + m
                dve.wait_ge(sq_ready, w + 1)
                nc.vector.tensor_reduce(neg_max[:, t, g * HG:(g + 1) * HG],
                                        sq_ps[w % 2][:, 0:GK].rearrange("p (h k) -> p h k", h=HG),
                                        AX.X, ALU.max, negate=True).then_inc(max_done, 1)

            def place_maximum(i):
                dve.wait_ge(max_done, (i + 1) * T * G)
                heads = neg_max[:].rearrange("p t (g h) -> p t g h", g=G)
                placed = max_st[:].rearrange("p t (g c) -> p t g c", g=G)
                chain(nc.vector.tensor_copy(placed[:, :, :, 0:HG], heads))
                nc.vector.tensor_tensor(placed[:, :, :, HG:2 * HG], heads, placed[:, :, :, 0:HG].bitcast(F32),
                                        ALU.subtract).then_inc(max_st_ready, 1)

            def store(n):
                dve.wait_ge(down_done, (n + 1) * NU)
                if n >= 2:
                    dve.wait_ge(out_done[n % 2], 16 * (n // 2))
                nc.vector.tensor_tensor(y_sb[:, n % 2].rearrange("p t d -> p (t d)"), acc[:],
                                        x2[:, n].rearrange("p t d -> p (t d)"), ALU.add).then_inc(y_ready, 1)

            def side_step(i, kind, g):
                b = i - 2
                if kind == "den":
                    k, n = misc_of("den", b, 0)
                    dve.wait_ge(misc_ready[k], n)
                    nc.vector.reciprocal(den_inv[:].rearrange("p t h -> p (t h)"),
                                         misc[k][:].rearrange("p (n d) -> p n d", d=HD)[:, :, 0])\
                        .then_inc(den_inv_ready, 1)
                    dve.wait_ge(den_inv_ready, b + 1)
                    nc.vector.tensor_copy(den_rep[:].rearrange("p t (h d) -> p (t h) d", d=HD),
                                          den_inv[:].rearrange("p t h -> p (t h)").unsqueeze(2)
                                          .to_broadcast([P, T * H, HD])).then_inc(den_rep_ready, 1)
                elif kind == "v":
                    k, n = misc_of("v", g, 0)
                    if g == 0:
                        dve.wait_ge(ld["v_mask"], 16)
                    dve.wait_ge(misc_ready[k], n)
                    for j, (a, z) in enumerate(KC):
                        ins = nc.vector.tensor_tensor(v_bd[0:z - a, g, j], misc[k][0:z - a, j * D:(j + 1) * D],
                                                      v_mask[0:z - a, j], ALU.mult)
                    ins.then_inc(v_bd_ready, 1)
                elif kind == "xt":
                    low_part(xt_lo[:], xt_hi[:], "xt", i, 0, hi_ready=xt_hi_ready, done=xt_lo_ready)
                elif kind == "q":
                    k, n = misc_of("q", i, g)
                    a = slice(QUAD * quads(g)[1], QUAD * quads(g)[1] + QUAD)
                    dve.wait_ge(q_hi_ready, i * G + g + 1)
                    nc.vector.scalar_tensor_tensor(
                        out=q_st[a, i % 2, g], in0=misc[k][a, 0:S], scalar=bq_sb[a, g:g + 1],
                        in1=q_st[a, i % 2, g].bitcast(F32), op0=ALU.add, op1=ALU.subtract).then_inc(q_lo_ready, 1)
                elif kind == "inv":
                    dve.wait_ge(inv_t_ready, b + 1)
                    nc.vector.tensor_tensor(att_t[:], po[:], inv_t[:], ALU.mult).then_inc(att_ready, 1)
                elif kind == "wo":
                    k, n = misc_of("wo", b, 0)
                    dve.wait_ge(misc_ready[k], n)
                    dve.wait_ge(x_bo_ready, b + 1)
                    nc.vector.tensor_tensor(x2[:, b].rearrange("p t d -> p (t d)"), misc[k][:],
                                            x_bo[:, b].rearrange("p t d -> p (t d)"), ALU.add)\
                        .then_inc(x2_ready, 1)
                    dve.wait_ge(x2_ready, b + 1)
                    moments(1, b, x2)
                elif kind == "x2t":
                    low_part(x2t_lo[:, b * S:(b + 1) * S], x2t_hi[:, b * S:(b + 1) * S], "x2t", b, 0,
                             hi_ready=x2t_hi_ready, done=x2t_lo_ready)
                elif kind == "norm":
                    normalise(1, b, x2)
                elif kind == "moments":
                    dve.wait_ge(ld_x[i + 1], 16)
                    moments(0, i + 1, x_sb)
                elif kind == "norm_next":
                    normalise(0, i + 1, x_sb)
                elif kind == "split_router":
                    dve.wait_ge(ld["rw"], 16)
                    chain(nc.vector.tensor_copy(rw_st[:, 0], rw_sb[:]))
                    nc.vector.tensor_tensor(rw_st[:, 1], rw_sb[:], rw_st[:, 0].bitcast(F32), ALU.subtract)\
                        .then_inc(rw_split, 1)
                elif kind == "route":
                    route(b)
                elif kind == "combine":
                    combine_weights(b)
                elif kind == "place_max":
                    place_maximum(i)
                elif kind == "store":
                    store(i - 3)

            dve.wait_ge(ld_x[0], 16)
            moments(0, 0, x_sb)
            dve.wait_ge(ld["wq"], 16)
            chain(nc.vector.tensor_copy(wq_hi[:], wq_sb[:]))
            nc.vector.tensor_tensor(wq_lo[:], wq_sb[:], wq_hi[:].bitcast(F32), ALU.subtract).then_inc(wq_split, 1)
            normalise(0, 0, x_sb)
            for g in range(G):
                k, n = misc_of("k", g, 0)
                a = slice(QUAD * quads(g)[2], QUAD * quads(g)[2] + QUAD)
                dve.wait_ge(k_hi_ready, g + 1)
                nc.vector.tensor_tensor(k_st[a, g], misc[k][a, 0:B * SK], k_st[a, g].bitcast(F32), ALU.subtract)\
                    .then_inc(k_st_ready, 1)
            dve.wait_ge(zeroed, 3)
            dve.wait_ge(ld["consts"], 16)
            for i, (slots, turns) in enumerate(PLAN):
                for p, here in enumerate(slots):
                    if i >= 3:
                        expert(i - 3, p)
                    for kind, g in here:
                        side_step(i, kind, g)
                for m in range(T * G + 1):
                    if i < B and m < T * G:
                        row_maximum(i, m)
                    for kind, g in turns[m]:
                        side_step(i, kind, g)

        @block.tensor
        def _(pe):
            def take(*use):
                if before[use]:
                    pe.wait_ge(*released(*before[use]))
                if use in st_first and scored[0]:
                    pe.wait_ge(exp_done, scored[0])
                k = bank_of[use]
                return misc[k], misc_ready[k]

            scored = [0]

            def transposes(src, *use):
                ps, ready = take(*use)
                for t in range(T):
                    ins = nc.tensor.transpose(ps[:, t * P:(t + 1) * P], src(t), ident)
                ins.then_inc(ready, 1)

            def side_step(i, kind, g):
                b = i - 2
                if kind == "max":
                    pe.wait_ge(max_st_ready, i)
                    transposes(lambda t: max_st[:, t].bitcast(F32), "max", i - 1, 0)
                elif kind == "den":
                    pe.wait_ge(den_copied, b + 1)
                    transposes(lambda t: den_sb[:, t * P:(t + 1) * P], "den", b, 0)
                elif kind == "v":
                    ps, ready = take("v", g, 0)
                    pe.wait_ge(ctx_rep_ready, g + 1)
                    if g == 0:
                        pe.wait_ge(ld["wv"], 16)
                    for j, (a, z) in enumerate(KC):
                        ins = nc.tensor.matmul(ps[0:z - a, j * D:(j + 1) * D],
                                               ctx_rep[:, g].rearrange("c h k -> c (h k)")[:, a:z], wv_sb[:],
                                               start=True, stop=True)
                    ins.then_inc(ready, 1)
                elif kind == "xt":
                    pe.wait_ge(xn_ready[0], i + 1)
                    transposes(lambda t: xn[:, 0, t], "xt", i, 0)
                elif kind == "q":
                    ps, ready = take("q", i, g)
                    if i == 0 and g == 0:
                        pe.wait_ge(wq_split, 1)
                    pe.wait_ge(xt_hi_ready, i + 1)
                    nc.tensor.matmul(ps[:, 0:S], wq_hi[:, g], xt_hi[:], start=True, stop=False)
                    nc.tensor.matmul(ps[:, 0:S], wq_lo[:, g], xt_hi[:], start=False, stop=False)
                    pe.wait_ge(xt_lo_ready, i + 1)
                    nc.tensor.matmul(ps[:, 0:S], wq_hi[:, g], xt_lo[:], start=False, stop=True).then_inc(ready, 1)
                elif kind == "inv":
                    pe.wait_ge(den_rep_ready, b + 1)
                    transposes(lambda t: den_rep[:, t], "inv", b, 0)
                elif kind == "wo":
                    ps, ready = take("wo", b, 0)
                    if b == 0:
                        pe.wait_ge(ld["wo"], 16)
                    pe.wait_ge(att_ready, b + 1)
                    for t in range(T):
                        ins = nc.tensor.matmul(ps[:, t * D:(t + 1) * D], att_t[:, t * P:(t + 1) * P], wo_sb[:],
                                               start=True, stop=True)
                    ins.then_inc(ready, 1)
                elif kind == "x2t":
                    pe.wait_ge(xn_ready[1], b + 1)
                    transposes(lambda t: xn[:, 1, t], "x2t", b, 0)
                elif kind == "router":
                    ps, ready = take("router", b, 0)
                    if b == 0:
                        pe.wait_ge(rw_split, 1)
                    pe.wait_ge(x2t_hi_ready, b + 1)
                    pe.wait_ge(x2t_lo_ready, b + 1)
                    for t in range(T):
                        tok = slice(b * S + t * P, b * S + (t + 1) * P)
                        nc.tensor.matmul(ps[:, t * 2 * E:t * 2 * E + E], x2t_lo[:, tok], rw_st[:, 0],
                                         start=True, stop=False, skip_group_check=True)
                        ins = nc.tensor.matmul(ps[:, t * 2 * E:(t + 1) * 2 * E], x2t_hi[:, tok],
                                               rw_st[:].rearrange("p a e -> p (a e)"), start=False, stop=True,
                                               skip_group_check=True)
                    ins.then_inc(ready, 1)
                elif kind == "comb":
                    pe.wait_ge(comb_st_ready, b + 1)
                    transposes(lambda t: comb_st[:, t].bitcast(F32), "comb", b, 0)

            def scores(i, m):
                t, g = m // G, m % G
                w = i * T * G + m
                if t == 0:
                    pe.wait_ge(q_lo_ready, i * G + g + 1)
                    pe.wait_ge(k_bd_ready, i * G + g + 1)
                if m < 2 and i >= 3:
                    pe.wait_ge(silu_done, (i - 2) * NU)
                if w >= 2:
                    pe.wait_ge(max_done, w - 1)
                nc.tensor.matmul(sq_ps[w % 2][:, 0:GK], q_st[:, i % 2, g, t * P:(t + 1) * P], k_bd[:, g, i],
                                 start=True, stop=True).then_inc(sq_ready, 1)

            def scores_t(b, m):
                j, g = m // G, m % G
                e = b * NJ * G + m
                a, z = KC[j]
                if j == 0:
                    pe.wait_ge(q_max_ready, b * G + g + 1)
                if m < 2 and b >= 2:
                    pe.wait_ge(hid_ready, (b - 1) * NU)
                if e >= 2:
                    pe.wait_ge(exp_done, e - 1)
                if m < 2 and b < 2 and st_last[b + 1][e % 2]:
                    pe.wait_ge(*released(*st_last[b + 1][e % 2]))
                scored[0] = e + 1
                nc.tensor.matmul(st_ps[e % 2][0:z - a, :], k_bd[:, g, b, a:z], q_st[:, b % 2, g],
                                 start=True, stop=True).then_inc(st_ready, 1)

            def weigh(b, j):
                a, z = KC[j]
                if j == 0:
                    pe.wait_ge(v_bd_ready, b + 1)
                    if b > 0:
                        pe.wait_ge(den_copied, b)
                        pe.wait_ge(att_ready, b)
                    if b >= 2:
                        pe.wait_ge(y_ready, b - 1)
                for out_ps, lhs in ((po, v_bd[0:z - a, b, j]), (pd, v_mask[0:z - a, j])):
                    for g in range(G):
                        e = b * NJ * G + j * G + g
                        pe.wait_ge(exp_done, e + 1)
                        q = slice(QUAD * g, QUAD * (g + 1))
                        ins = nc.tensor.matmul(out_ps[q, :], lhs[:, q], probs[0:z - a, e % 8],
                                               start=(j == 0), stop=(j == NJ - 1))
                ins.then_inc(pv_done, 1)

            def gate_up(n, p):
                u = n * NU + p
                tok = slice(n * S, (n + 1) * S)
                for ps, hi, lo, ready, read in ((gate_ps, wg_hi, wg_lo, gate_ready, gate_read),
                                                (up_ps, wu_hi, wu_lo, up_ready, up_read)):
                    if p >= 2:
                        pe.wait_ge(*read(u - 2))
                    elif ps is gate_ps:
                        pe.wait_ge(max_done, min(n + 3, B) * T * G)
                    else:
                        pe.wait_ge(exp_done, min(n + 2, B) * NJ * G)
                    nc.tensor.matmul(ps[p % 2][:], hi[:, p], x2t_hi[:, tok], start=True, stop=False)
                    nc.tensor.matmul(ps[p % 2][:], hi[:, p], x2t_lo[:, tok], start=False, stop=False)
                    nc.tensor.matmul(ps[p % 2][:], lo[:, p], x2t_hi[:, tok], start=False, stop=True)\
                        .then_inc(ready, 1)
                if p < NP:
                    ps, ready = take("spread", n, p)
                    if p == 0:
                        pe.wait_ge(comb_t_ready, n + 1)
                    nc.tensor.matmul(ps[:], sel[:, 2 * p:2 * p + 2].rearrange("p e f -> p (e f)"),
                                     comb_t[:, tok], start=True, stop=True).then_inc(ready, 1)

            def down_proj(n, p):
                u = n * NU + p
                if p == 0:
                    pe.wait_ge(den_copied, min(n + 2, B))
                    if n > 0:
                        pe.wait_ge(y_ready, n)
                pe.wait_ge(hid_ready, u + 1)
                for t in range(T):
                    ins = nc.tensor.matmul(acc[:, t * D:(t + 1) * D], hid[:, u % 3, t * P:(t + 1) * P],
                                           wd_sb[:, p], start=(p == 0 and t == 0), stop=(p == NU - 1),
                                           skip_group_check=True)
                ins.then_inc(down_done, 1)

            pe.wait_ge(ld["ctx"], 16)
            pe.wait_ge(ld["wk"], 16)
            for g in range(G):
                ps, ready = take("k", g, 0)
                nc.tensor.matmul(ps[:, 0:B * SK], wk_sb[:, g], ctx_sb[:].rearrange("c b k -> c (b k)"),
                                 start=True, stop=True).then_inc(ready, 1)
            pe.wait_ge(ld["consts"], 16)
            for i, (slots, turns) in enumerate(PLAN):
                if i == 3:
                    pe.wait_ge(w_lo_ready, 2)
                    pe.wait_ge(sel_ready, 1)
                    pe.wait_ge(ld["wd"], 32)
                for p, here in enumerate(slots):
                    if i >= 3:
                        gate_up(i - 3, p)
                        if p > 0:
                            down_proj(i - 3, p - 1)
                    for kind, g in here:
                        side_step(i, kind, g)
                if i >= 3:
                    down_proj(i - 3, NU - 1)
                for m in range(T * G + 1):
                    if i < B and m < T * G:
                        scores(i, m)
                    if 0 <= i - 1 < B and m < NJ * G:
                        scores_t(i - 1, m)
                    if 0 <= i - 1 < B and m in (6, 10, 14):
                        weigh(i - 1, (m - 6) // G)
                    for kind, g in turns[m]:
                        side_step(i, kind, g)


_ARGS = ["x", "ctx_t", "wq", "bq", "wk", "wv", "wo", "bo", "router_t", "router_bias", "up", "gate", "down",
         "sh_gate_t", "sh_up_t", "sh_down_t", "consts", "v_mask"]


def kernel(**inputs):
    import numpy as np
    from concourse import bacc
    from concourse.bass_utils import run_bass_kernel_spmd

    a = {n.replace("L0_xattn_", "").replace("L0_ffn_", ""): np.asarray(v) for n, v in inputs.items()}
    x, y = a["x"], a["ctx_768"]
    B, SK, C = y.shape
    D = x.shape[2]
    E = a["up_proj"].shape[0]
    QUAD, G, HG, P = 32, 4, 4, 128
    HD = D // (G * HG)
    chunks = [(0, 104), (104, 206), (206, 308)]

    ctx_t = np.ones((C + 1, B, SK), x.dtype)
    ctx_t[:C] = y.transpose(2, 0, 1)
    wq = np.zeros((D, G, P), x.dtype)
    bq = np.zeros((P, G), x.dtype)
    wk = np.zeros((C + 1, G, P), x.dtype)
    for g in range(G):
        cols = slice(QUAD * g, QUAD * (g + 1))
        for a4 in range(4):
            here = slice(QUAD * a4, QUAD * (a4 + 1))
            if a4 != g:
                wq[:, g, here] = a["wq"][:, cols]
                bq[here, g] = a["bq"][cols]
                wk[:C, g, here] = a["wk"][:, cols]
                wk[C, g, here] = a["bk"][cols]
            else:
                wk[C, g, here] = 1.0
    wv = np.concatenate([a["wv"], a["bv"][None]], 0)

    row = np.arange(P)
    k_mask = np.zeros((P, G, HG), x.dtype)
    for g in range(G):
        for h in range(HG):
            k_mask[:, g, h] = (row % QUAD) // HD == h
            own = row // QUAD == g
            k_mask[own, g, h] = ((row % QUAD) % HG == h)[own] & ((row % QUAD) < 2 * HG)[own]
    v_mask = np.zeros((P, len(chunks), D), x.dtype)
    for j, (lo, hi) in enumerate(chunks):
        for r in range(hi - lo):
            v_mask[r, j] = (np.arange(D) % QUAD) // HD == (lo + r) // SK
    pair_rows = np.zeros((P, E), x.dtype)
    for e in range(E):
        pair_rows[e, e] = pair_rows[QUAD + e, e] = 1.0
    iota = np.tile(np.arange(E, dtype=x.dtype), (P, 1))
    consts = np.concatenate([np.eye(P, dtype=x.dtype), k_mask.reshape(P, -1), pair_rows, iota], 1)

    laid = {
        "x": x, "ctx_t": ctx_t, "wq": wq, "bq": bq, "wk": wk, "wv": wv, "wo": a["wo"], "bo": a["bo"],
        "router_t": a["router_w"].T, "router_bias": a["router_bias"], "up": a["up_proj"], "gate": a["gate_proj"],
        "down": a["down_proj"], "sh_gate_t": a["sh_gate"].T, "sh_up_t": a["sh_up"].T, "sh_down_t": a["sh_down"].T,
        "consts": consts, "v_mask": v_mask,
    }
    nc = bacc.Bacc("TRN2", target_bir_lowering=False, num_devices=1)
    arrays, aps = {}, []
    for name in _ARGS:
        arr = np.ascontiguousarray(laid[name])
        arrays[f"in_{name}"] = arr
        aps.append(nc.dram_tensor(f"in_{name}", arr.shape, mybir.dt.from_np(arr.dtype), kind="ExternalInput").ap())
    aps.append(nc.dram_tensor("out_y", x.shape, F32, kind="ExternalOutput").ap())
    build(nc, *aps)
    r = run_bass_kernel_spmd(nc, [arrays], core_ids=[0])
    return r.results[0]["out_y"]
```

```python
from contextlib import ExitStack

import concourse.bass as bass
from concourse import mybir

F32 = mybir.dt.float32
F32R = mybir.dt.float32r
U32 = mybir.dt.uint32
ALU = mybir.AluOpType
ACT = mybir.ActivationFunctionType
AX = mybir.AxisListType

P = 128
QUAD = 32
EPS = 1e-5


def build(nc, x, ctx_t, wq, bq, wk, wv, wo, bo, router_t, router_bias, up, gate, down,
          sh_gate_t, sh_up_t, sh_down_t, consts, v_mask_c, out):
    B, S, D = x.shape
    H, HD = 16, D // 16
    G, HG = 4, 4
    SK = ctx_t.shape[2]
    C1 = ctx_t.shape[0]
    GK = HG * SK
    KC = [(0, 104), (104, 206), (206, 308)]
    NJ = len(KC)
    T = S // P
    E, _, F = up.shape
    NP = E // 2
    NU = NP + 1
    SCALE = float(HD) ** -0.5
    assert D == P and GK == KC[-1][1] and 2 * F == P and HG * HD == QUAD

    ctx = ExitStack()
    with ctx:
        def sb(name, shape, dt=F32):
            return ctx.enter_context(nc.sbuf_tensor(name, shape, dt))

        def sem(name):
            return ctx.enter_context(nc.semaphore(name))

        x_sb = sb("x_sb", [P, B, T, D])
        x2 = sb("x2", [P, B, T, D])
        ctx_sb = sb("ctx_sb", [C1, B, SK])
        ctx_rep = sb("ctx_rep", [C1, B, HG, SK])
        cst = sb("cst", [P, consts.shape[1]])
        ident = cst[:, 0:P]
        k_mask = cst[:, P:P + G * HG].rearrange("p (g h) -> p g h", g=G)
        pair_rows = cst[:, P + G * HG:P + G * HG + E]
        iota = cst[:, P + G * HG + E:P + G * HG + 2 * E]
        v_mask = sb("v_mask", [P, NJ, D])
        wq_sb = sb("wq_sb", [P, D])
        wq_hi = sb("wq_hi", [P, D], F32R)
        wq_lo = sb("wq_lo", [P, D], F32R)
        bq_sb = sb("bq_sb", [P, 1])
        place = sb("place", [P, 2, G, P], F32R)
        q_hi = sb("q_hi", [P, S], F32R)
        q_lo = sb("q_lo", [P, S], F32R)
        wk_sb = sb("wk_sb", [C1, G, P])
        wv_sb = sb("wv_sb", [C1, D])
        wo_sb = sb("wo_sb", [P, D])
        bo_sb = sb("bo_sb", [P, D])
        rw_sb = sb("rw_sb", [P, E])
        rw_st = sb("rw_st", [P, 2, E], F32R)
        rb_sb = sb("rb_sb", [P, E])
        wg_sb = sb("wg_sb", [P, NU, P])
        wu_sb = sb("wu_sb", [P, NU, P])
        wg_hi = sb("wg_hi", [P, NU, P], F32R)
        wg_lo = sb("wg_lo", [P, NU, P], F32R)
        wu_hi = sb("wu_hi", [P, NU, P], F32R)
        wu_lo = sb("wu_lo", [P, NU, P], F32R)
        wd_sb = sb("wd_sb", [P, NU, D])
        sel = sb("sel", [P, E, F], F32R)

        k_st = sb("k_st", [P, G, B * SK], F32R)
        k_bd = sb("k_bd", [P, G, B, GK], F32R)
        v_bd = sb("v_bd", [P, B, NJ, D])
        stats = sb("stats", [P, 2, T, 6])
        mean_var = sb("mean_var", [P, 2, T, 2])
        var_eps = sb("var_eps", [P, 2, T])
        rstd = sb("rstd", [P, 2, T])
        minus_half = sb("minus_half", [P, T])
        xn = sb("xn", [P, 2, T, D])
        xt_hi = sb("xt_hi", [P, S], F32R)
        xt_lo = sb("xt_lo", [P, S], F32R)
        q_st = sb("q_st", [P, 2, G, S], F32R)
        neg_max = sb("neg_max", [P, T, H])
        max_st = sb("max_st", [P, T, P], F32R)
        probs = sb("probs", [P, 8, S])
        den_sb = sb("den_sb", [P, S])
        den_inv = sb("den_inv", [P, T, H])
        den_rep = sb("den_rep", [P, T, D])
        inv_t = sb("inv_t", [P, S])
        att_t = sb("att_t", [P, S])
        x2t_hi = sb("x2t_hi", [P, B * S], F32R)
        x2t_lo = sb("x2t_lo", [P, B * S], F32R)
        logits = sb("logits", [P, T, E])
        top_v = sb("top_v", [P, T, 8])
        top_i = sb("top_i", [P, T, 8], U32)
        top_f = sb("top_f", [P, T, 2])
        gap = sb("gap", [P, T])
        gap_exp = sb("gap_exp", [P, T])
        gap_sum = sb("gap_sum", [P, T])
        top_w = sb("top_w", [P, T, 2])
        picked = sb("picked", [P, T, 2, E])
        combine = sb("combine", [P, T, E])
        comb_st = sb("comb_st", [P, T, P], F32R)
        comb_t = sb("comb_t", [P, B * S], F32R)
        silu = sb("silu", [P, 2, S])
        hid_u = sb("hid_u", [P, 2, S])
        hid = sb("hid", [P, 3, S])
        y_sb = sb("y_sb", [P, 2, T, D])

        banks = [ctx.enter_context(nc.psum_tensor(f"bank{i}", [P, 512], F32)) for i in range(8)]
        po, pd = banks[6], banks[7]

        names = ("consts", "v_mask", "ctx", "wk", "wv", "wq", "bq", "wo", "bo", "rw", "rb", "wgu", "wd")
        ld = {n: sem(f"ld_{n}") for n in names}
        ld_x = [sem(f"ld_x{b}") for b in range(B)]
        bank_ready = [sem(f"bank{k}_ready") for k in range(6)]
        dve_step = sem("dve_step")
        var_ready = [sem("var1_ready"), sem("var2_ready")]
        rstd_ready = [sem("rstd1_ready"), sem("rstd2_ready")]
        picked_ready = sem("picked_ready")
        zeroed = sem("zeroed")
        ctx_rep_ready = sem("ctx_rep_ready")
        wq_split = sem("wq_split")
        rw_split = sem("rw_split")
        k_hi_ready = sem("k_hi_ready")
        k_st_ready = sem("k_st_ready")
        k_bd_ready = sem("k_bd_ready")
        v_bd_ready = sem("v_bd_ready")
        stats_ready = [sem("stats1_ready"), sem("stats2_ready")]
        xn_ready = [sem("xn1_ready"), sem("xn2_ready")]
        x_bo_ready = sem("x_bo_ready")
        xt_hi_ready = sem("xt_hi_ready")
        xt_lo_ready = sem("xt_lo_ready")
        q_hi_ready = sem("q_hi_ready")
        q_lo_ready = sem("q_lo_ready")
        place_ready = sem("place_ready")
        q_st_ready = sem("q_st_ready")
        max_done = sem("max_done")
        max_st_ready = sem("max_st_ready")
        q_max_ready = sem("q_max_ready")
        exp_done = sem("exp_done")
        pv_done = sem("pv_done")
        den_copied = sem("den_copied")
        den_inv_ready = sem("den_inv_ready")
        den_rep_ready = sem("den_rep_ready")
        inv_t_ready = sem("inv_t_ready")
        att_ready = sem("att_ready")
        x2_ready = sem("x2_ready")
        x2t_hi_ready = sem("x2t_hi_ready")
        x2t_lo_ready = sem("x2t_lo_ready")
        router_read = sem("router_read")
        gap_ready = sem("gap_ready")
        gap_exp_ready = sem("gap_exp_ready")
        comb_st_ready = sem("comb_st_ready")
        comb_t_ready = sem("comb_t_ready")
        w_hi_ready = sem("w_hi_ready")
        w_lo_ready = sem("w_lo_ready")
        sel_ready = sem("sel_ready")
        silu_done = sem("silu_done")
        hid_u_done = sem("hid_u_done")
        hid_ready = sem("hid_ready")
        down_done = sem("down_done")
        y_ready = sem("y_ready")
        out_done = [sem("out_done_even"), sem("out_done_odd")]

        ORDER = """
            norm0 ctx_rep0 k0 k1 k2 moments1 k_bd0 xt0 k3 q0 place_q0 norm1 place_q0 k_bd1
            place_q0*2 sq0 ctx_rep1 sq0*2 ctx_rep2 sq0*3 xt1 sq0*2 v0 q1 sq0 k_bd2 sq0*2 place_q1
            sq0*2 place_q1 sq0*3 place_max0 place_q1 v1 sq1 ctx_rep3 place_q1 sq1*2 x_bo0 max0 v2 v3
            st0 sq1*2 st0 sq1 st0 sq1*2 st0*2 split_gate0 st0 moments2 st0 sq1 sel0 weigh0 st0 sq1*2
            st0*2 sq1 weigh0 sq1 split_router0 sq1 x_bo1 st0 sq1 st0 sq1 place_max1 weigh0 split_up0
            den_copy0 max1 norm2 den0 xt2 st1 inv0 st1 q2 st1*3 wo0 st1 place_q2*2 midnorm0 place_q2
            st1 weigh1 st1 place_q2 st1 sq2 st1 x2t0 weigh1 st1 sq2 route0 combine0 router0 st1
            gap_exp0 unit0 sq2*3 den_copy1 weigh1 comb0 unit0 down0 sq2 den1 sq2 unit0 inv1 unit0
            sq2 x_bo2 sq2 down0 sq2 wo1 unit0 sq2 down0 sq2*2 down0 midnorm1 unit0 down0 sq2*2 unit0
            k_bd3 sq2 down0 place_max2 unit0 x2t1 moments3 unit0 max2 unit1 down0 st2 down0*2 st2
            norm3 st2*2 router1 st2*3 store0 gap_exp1 route1 st2 xt3 weigh2 combine1 st2*3 q3 weigh2
            comb1 st2 place_q3*4 sq3 weigh2 unit1 sq3*3 den_copy2 sq3 down1 unit1 sq3*3 den2 down1
            unit1 sq3*3 down1 sq3 unit1 inv2 unit1 sq3 down1 sq3 wo2 sq3*2 place_max3 unit1 down1
            midnorm2 unit1 max3 down1*2 x2t2 unit1 st3*2 router2 st3*2 route2 gap_exp2 combine2
            st3*2 x_bo3 st3 down1 st3*2 down1 st3*3 store1 comb2 weigh3*2 den_copy3 weigh3 unit2
            den3 unit2 down2 inv3 unit2 down2 wo3 unit2 midnorm3 down2 unit2 down2 x2t3 unit2 down2
            unit2 route3 router3 unit2*2 gap_exp3 down2 combine3 unit3 store2 down2*3 comb3 unit3
            down3 unit3*2 down3*3 unit3*3 down3*2 unit3*2 down3*3 store3
            """
        PLAN = []
        for word in ORDER.split():
            step, _, times = word.partition("*")
            kind, b = step[:-1], int(step[-1])
            for _ in range(int(times or 1)):
                PLAN.append((kind, b, sum(1 for s in PLAN if s[:2] == (kind, b))))

        SINGLE = ("k", "v", "xt", "q", "place_q", "max", "den", "inv", "wo", "x2t", "router", "comb", "sq", "st")
        uses, bank_of, count_of, before = [], {}, {}, {}
        last_on = [None] * 6
        filled = [0] * 6
        for kind, b, g in PLAN:
            for use in ([("gate", b, g), ("up", b, g), ("spread", b, g)][:3 if g > 0 else 2] if kind == "unit" else
                        [(kind, b, g)] if kind in SINGLE else []):
                k = len(uses) % 6
                before[use] = last_on[k]
                last_on[k] = use
                filled[k] += 1
                bank_of[use], count_of[use] = k, filled[k]
                uses.append(use)

        def bank(*use):
            return banks[bank_of[use]]

        def filled_by(*use):
            return bank_ready[bank_of[use]], count_of[use]

        def released(kind, b, g):
            if kind == "up":
                return (hid_u_done, b * NP + g) if g > 0 else (hid_ready, b * NU + 1)
            return {"k": (k_st_ready, b + 1), "v": (v_bd_ready, b + 1), "comb": (comb_t_ready, b + 1),
                    "den": (den_inv_ready, b + 1), "xt": (xt_lo_ready, b + 1),
                    "q": (q_lo_ready, b + 1), "place_q": (q_st_ready, b * G + g + 1),
                    "inv": (inv_t_ready, b + 1), "wo": (x2_ready, b + 1), "x2t": (x2t_lo_ready, b + 1),
                    "max": (q_max_ready, (b + 1) * G), "router": (router_read, b + 1),
                    "sq": (max_done, b * T * G + g + 1), "st": (exp_done, b * NJ * G + g + 1),
                    "gate": (silu_done, b * NU + g + 1), "spread": (hid_ready, b * NU + g + 1)}[kind]

        weighed_before = {n: sum(1 for s in PLAN[:PLAN.index(("down", n, 0))] if s[0] == "den_copy")
                          for n in range(B)}
        stored_before = {b: sum(1 for s in PLAN[:PLAN.index(("weigh", b, 0))] if s[0] == "store")
                         for b in range(B)}

        def shares(u):
            return [slice(0, S // 2), slice(S // 2, S)] if u == B * NU - 1 else [slice(0, S)]

        def acc_of(n, t):
            return po if n == B - 1 and t >= T // 2 else pd

        def quads(g):
            return [a for a in range(4) if a != g]

        block = ctx.enter_context(nc.Block())

        @block.sync
        def _(sp):
            sp.dma_start(ctx_sb[:], ctx_t).then_inc(ld["ctx"], 16)
            sp.dma_start(wk_sb[:], wk).then_inc(ld["wk"], 16)
            sp.dma_start(cst[:], consts).then_inc(ld["consts"], 16)
            sp.dma_start(bq_sb[:], bq).then_inc(ld["bq"], 16)
            sp.dma_start(wv_sb[:], wv).then_inc(ld["wv"], 16)
            sp.dma_start(v_mask[:], v_mask_c).then_inc(ld["v_mask"], 16)
            for b in range(1, B):
                sp.dma_start(x_sb[:, b], x[b].rearrange("(t p) d -> p t d", p=P)).then_inc(ld_x[b], 16)
            sp.dma_start(bo_sb[:], bo.partition_broadcast(P)).then_inc(ld["bo"], 16)
            sp.dma_start(wo_sb[:], wo).then_inc(ld["wo"], 16)
            sp.dma_start(rw_sb[:], router_t).then_inc(ld["rw"], 16)
            sp.dma_start(rb_sb[:], router_bias.partition_broadcast(P)).then_inc(ld["rb"], 16)
            sp.dma_start(wg_sb[:, 1:NU, :].rearrange("p n (a f) -> p (n a) f", a=2),
                         gate.rearrange("e d f -> d e f")).then_inc(ld["wgu"], 16)
            sp.dma_start(wg_sb[:, 0, :], sh_gate_t).then_inc(ld["wgu"], 16)
            sp.dma_start(wu_sb[:, 1:NU, :].rearrange("p n (a f) -> p (n a) f", a=2),
                         up.rearrange("e d f -> d e f")).then_inc(ld["wgu"], 16)
            sp.dma_start(wu_sb[:, 0, :], sh_up_t).then_inc(ld["wgu"], 16)
            sp.dma_start(wd_sb[:, 1:NU, :], down.rearrange("(n a) f d -> (a f) n d", a=2)).then_inc(ld["wd"], 16)
            sp.dma_start(wd_sb[:, 0, :], sh_down_t).then_inc(ld["wd"], 16)
            for n in range(B):
                for k, tok in enumerate(shares((n + 1) * NU - 1)):
                    sp.wait_ge(y_ready, n + 1 + k)
                    tiles = slice(tok.start // P, tok.stop // P)
                    sp.dma_start(out[n].rearrange("(t p) d -> p t d", p=P)[:, tiles], y_sb[:, n % 2, tiles])\
                        .then_inc(out_done[n % 2], 16)
            sp.wait_ge(out_done[0], 16 * (B // 2))
            sp.wait_ge(out_done[1], 16 * (B // 2 + 1))

        @block.gpsimd
        def _(pool):
            def inverse_root(which, n):
                pool.wait_ge(stats_ready[which], n + 1)
                nc.gpsimd.tensor_scalar(var_eps[:, which], mean_var[:, which, :, 1], EPS, None, ALU.add)\
                    .then_inc(var_ready[which], 1)
                pool.wait_ge(var_ready[which], n + 1)
                nc.gpsimd.tensor_tensor(rstd[:, which], var_eps[:, which], minus_half[:], ALU.pow)\
                    .then_inc(rstd_ready[which], 1)

            def expand_k(b):
                for g in range(G):
                    if b == 0:
                        pool.wait_ge(k_st_ready, g + 1)
                    keys = k_st[:, g, b * SK:(b + 1) * SK].bitcast(F32)
                    nc.gpsimd.tensor_tensor(
                        k_bd[:, g, b].rearrange("p (h k) -> p h k", h=HG),
                        keys.unsqueeze(1).to_broadcast([P, HG, SK]),
                        k_mask[:, g].unsqueeze(2).to_broadcast([P, HG, SK]), ALU.mult).then_inc(k_bd_ready, 1)

            def add_bo(b):
                pool.wait_ge(ld_x[b], 16)
                nc.gpsimd.tensor_tensor(x2[:, b], x_sb[:, b], bo_sb[:].unsqueeze(1).to_broadcast([P, T, D]),
                                        ALU.add).then_inc(x_bo_ready, 1)

            nc.gpsimd.memset(minus_half[:], -0.5).then_inc(zeroed, 1)
            nc.gpsimd.memset(max_st[:].bitcast(F32), 0.0).then_inc(zeroed, 1)
            nc.gpsimd.memset(comb_st[:].bitcast(F32), 0.0).then_inc(zeroed, 1)
            nc.gpsimd.memset(place[:].bitcast(F32), 0.0).then_inc(zeroed, 1)
            pool.wait_ge(zeroed, 4)
            inverse_root(0, 0)
            pool.wait_ge(ld["consts"], 16)
            for g in range(G):
                rows = slice(QUAD * g, QUAD * (g + 1))
                for part, a in zip((0, 1, 0), quads(g)):
                    ins = nc.gpsimd.tensor_copy(place[:, part, g, QUAD * a:QUAD * (a + 1)], ident[:, rows])
                ins.then_inc(place_ready, 1)
            for kind, b, g in PLAN:
                if kind == "moments":
                    inverse_root(0, b)
                elif kind == "wo":
                    inverse_root(1, b)
                elif kind == "k_bd":
                    if b == 0:
                        pool.wait_ge(ld["consts"], 16)
                    expand_k(b)
                elif kind == "x_bo":
                    if b == 0:
                        pool.wait_ge(ld["bo"], 16)
                    add_bo(b)
                elif kind == "sel":
                    nc.gpsimd.tensor_copy(sel[:], pair_rows.unsqueeze(2).to_broadcast([P, E, F]))\
                        .then_inc(sel_ready, 1)
                elif kind == "split_gate":
                    pool.wait_ge(w_hi_ready, 1)
                    nc.gpsimd.tensor_tensor(wg_lo[:], wg_sb[:], wg_hi[:].bitcast(F32), ALU.subtract)\
                        .then_inc(w_lo_ready, 1)
                elif kind == "split_up":
                    pool.wait_ge(w_hi_ready, 2)
                    nc.gpsimd.tensor_tensor(wu_lo[:], wu_sb[:], wu_hi[:].bitcast(F32), ALU.subtract)\
                        .then_inc(w_lo_ready, 1)

        @block.scalar
        def _(act):
            def copy_bank(dst, *use, done):
                act.wait_ge(*filled_by(*use))
                nc.scalar.activation(dst, bank(*use)[:, 0:dst.shape[-1]], ACT.Copy).then_inc(done, 1)

            act.dma_start(x_sb[:, 0], x[0].rearrange("(t p) d -> p t d", p=P)).then_inc(ld_x[0], 16)
            act.dma_start(wq_sb[:], wq).then_inc(ld["wq"], 16)
            for kind, b, g in PLAN:
                if kind == "k":
                    copy_bank(k_st[:, b], "k", b, 0, done=k_hi_ready)
                elif kind == "xt":
                    copy_bank(xt_hi[:], "xt", b, 0, done=xt_hi_ready)
                elif kind == "q":
                    act.wait_ge(*filled_by("q", b, g))
                    if b == 0:
                        act.wait_ge(ld["bq"], 16)
                    nc.scalar.activation(q_hi[:], bank("q", b, g)[:, 0:S], ACT.Identity,
                                         bias=bq_sb[:]).then_inc(q_hi_ready, 1)
                elif kind == "place_q":
                    copy_bank(q_st[:, b % 2, g], "place_q", b, g, done=q_st_ready)
                elif kind == "ctx_rep":
                    if b == 0:
                        act.wait_ge(ld["ctx"], 16)
                    nc.scalar.activation(ctx_rep[:, b], ctx_sb[:, b].unsqueeze(1).to_broadcast([C1, HG, SK]),
                                         ACT.Copy).then_inc(ctx_rep_ready, 1)
                elif kind == "max":
                    act.wait_ge(*filled_by("max", b, 0))
                    for g in range(G):
                        a = slice(QUAD * g, QUAD * (g + 1))
                        nc.scalar.activation(q_st[a, b % 2, g], bank("max", b, 0)[a, 0:S], ACT.Copy)\
                            .then_inc(q_max_ready, 1)
                elif kind == "st":
                    e = b * NJ * G + g
                    rows = KC[g // G][1] - KC[g // G][0]
                    act.wait_ge(*filled_by("st", b, g))
                    if e >= 8:
                        act.wait_ge(pv_done, (e - 8) // G + 1)
                    nc.scalar.activation(probs[0:rows, e % 8], bank("st", b, g)[0:rows, :], ACT.Exp,
                                         scale=SCALE).then_inc(exp_done, 1)
                elif kind == "den_copy":
                    act.wait_ge(pv_done, NJ * (b + 1))
                    if b > 0:
                        act.wait_ge(*filled_by("den", b - 1, 0))
                    nc.scalar.activation(den_sb[:], pd[:], ACT.Copy).then_inc(den_copied, 1)
                elif kind == "inv":
                    copy_bank(inv_t[:], "inv", b, 0, done=inv_t_ready)
                elif kind == "x2t":
                    copy_bank(x2t_hi[:, b * S:(b + 1) * S], "x2t", b, 0, done=x2t_hi_ready)
                elif kind == "gap_exp":
                    act.wait_ge(gap_ready, b + 1)
                    nc.scalar.activation(gap_exp[:], gap[:], ACT.Exp).then_inc(gap_exp_ready, 1)
                elif kind == "comb":
                    copy_bank(comb_t[:, b * S:(b + 1) * S], "comb", b, 0, done=comb_t_ready)
                elif kind == "split_gate":
                    act.wait_ge(ld["wgu"], 64)
                    nc.scalar.activation(wg_hi[:], wg_sb[:], ACT.Copy).then_inc(w_hi_ready, 1)
                elif kind == "split_up":
                    nc.scalar.activation(wu_hi[:], wu_sb[:], ACT.Copy).then_inc(w_hi_ready, 1)
                elif kind == "unit":
                    u = b * NU + g
                    act.wait_ge(*filled_by("gate", b, g))
                    if u >= 2:
                        act.wait_ge(*released("up", *divmod(u - 2, NU)))
                    nc.scalar.activation(silu[:, u % 2], bank("gate", b, g)[:], ACT.Silu).then_inc(silu_done, 1)

        @block.vector
        def _(dve):
            steps = [0]

            def chain(ins):
                ins.then_inc(dve_step, 1)
                steps[0] += 1
                dve.wait_ge(dve_step, steps[0])

            def moments(which, n, src):
                for t in range(T):
                    ins = nc.vector.bn_stats(stats[:, which, t], src[:, n, t])
                chain(ins)
                for t in range(T):
                    ins = nc.vector.bn_aggr(mean_var[:, which, t], stats[:, which, t])
                ins.then_inc(stats_ready[which], 1)

            def normalise(which, n, src):
                dve.wait_ge(rstd_ready[which], n + 1)
                if n > 0:
                    dve.wait_ge(*filled_by(("xt", "x2t")[which], n - 1, 0))
                for t in range(T):
                    ins = nc.vector.tensor_scalar(xn[:, which, t], src[:, n, t], mean_var[:, which, t, 0:1],
                                                  rstd[:, which, t:t + 1], ALU.subtract, ALU.mult)
                ins.then_inc(xn_ready[which], 1)

            def low_part(dst, hi, *use, hi_ready, done):
                dve.wait_ge(hi_ready, use[1] + 1)
                nc.vector.tensor_tensor(dst, bank(*use)[:, 0:S], hi.bitcast(F32), ALU.subtract).then_inc(done, 1)

            def expert(n, p):
                u = n * NU + p
                dve.wait_ge(silu_done, u + 1)
                dve.wait_ge(*filled_by("up", n, p))
                if u >= 3:
                    dve.wait_ge(down_done, u - 2)
                if p == 0:
                    nc.vector.tensor_tensor(hid[:, u % 3], bank("up", n, p)[:], silu[:, u % 2], ALU.mult)\
                        .then_inc(hid_ready, 1)
                for k, tok in enumerate(shares(u) if p > 0 else []):
                    nc.vector.tensor_tensor(hid_u[:, u % 2, tok], bank("up", n, p)[:, tok], silu[:, u % 2, tok],
                                            ALU.mult).then_inc(hid_u_done, 1)
                    dve.wait_ge(hid_u_done, n * NP + p + k)
                    if k == 0:
                        dve.wait_ge(*filled_by("spread", n, p))
                    nc.vector.tensor_tensor(hid[:, u % 3, tok], bank("spread", n, p)[:, tok], hid_u[:, u % 2, tok],
                                            ALU.mult).then_inc(hid_ready, 1)

            def route(b):
                dve.wait_ge(*filled_by("router", b, 0))
                if b == 0:
                    dve.wait_ge(ld["rb"], 16)
                parts = bank("router", b, 0)[:, 0:T * 2 * E].rearrange("p (t a e) -> p t a e", a=2, e=E)
                chain(nc.vector.tensor_tensor(logits[:], parts[:, :, 0], rb_sb[:].unsqueeze(1)
                                              .to_broadcast([P, T, E]), ALU.add))
                nc.vector.tensor_tensor(logits[:], parts[:, :, 1], logits[:], ALU.add).then_inc(router_read, 1)
                dve.wait_ge(router_read, b + 1)
                for t in range(T):
                    ins = nc.vector.max(top_v[:, t], logits[:, t])
                chain(ins)
                nc.vector.tensor_tensor(gap[:], top_v[:, :, 1], top_v[:, :, 0], ALU.subtract)\
                    .then_inc(gap_ready, 1)
                for t in range(T):
                    ins = nc.vector.max_index(top_i[:, t], top_v[:, t], logits[:, t])
                chain(ins)
                chain(nc.vector.tensor_copy(top_f[:], top_i[:, :, 0:2]))
                nc.vector.tensor_tensor(
                    picked[:], iota.unsqueeze(1).to_broadcast([P, 2 * T, E])
                    .rearrange("p (t a) e -> p t a e", a=2),
                    top_f[:].unsqueeze(3).to_broadcast([P, T, 2, E]), ALU.is_equal).then_inc(picked_ready, 1)

            def combine_weights(b):
                dve.wait_ge(gap_exp_ready, b + 1)
                chain(nc.vector.tensor_scalar(gap_sum[:], gap_exp[:], 1.0, None, ALU.add))
                chain(nc.vector.reciprocal(top_w[:, :, 0], gap_sum[:]))
                chain(nc.vector.tensor_tensor(top_w[:, :, 1], gap_exp[:], top_w[:, :, 0], ALU.mult))
                dve.wait_ge(picked_ready, b + 1)
                chain(nc.vector.tensor_tensor(picked[:], picked[:],
                                              top_w[:].unsqueeze(3).to_broadcast([P, T, 2, E]), ALU.mult))
                chain(nc.vector.tensor_tensor(combine[:], picked[:, :, 0], picked[:, :, 1], ALU.add))
                chain(nc.vector.tensor_copy(comb_st[:, :, 0:E], combine[:]))
                nc.vector.tensor_tensor(comb_st[:, :, QUAD:QUAD + E], combine[:],
                                        comb_st[:, :, 0:E].bitcast(F32), ALU.subtract).then_inc(comb_st_ready, 1)

            def row_maximum(b, m):
                t, g = m // G, m % G
                if b > 0 and m == 0:
                    dve.wait_ge(max_st_ready, b)
                dve.wait_ge(*filled_by("sq", b, m))
                nc.vector.tensor_reduce(neg_max[:, t, g * HG:(g + 1) * HG],
                                        bank("sq", b, m)[:, 0:GK].rearrange("p (h k) -> p h k", h=HG),
                                        AX.X, ALU.max, negate=True).then_inc(max_done, 1)

            def place_maximum(b):
                dve.wait_ge(max_done, (b + 1) * T * G)
                if b > 0:
                    dve.wait_ge(*filled_by("max", b - 1, 0))
                heads = neg_max[:].rearrange("p t (g h) -> p t g h", g=G)
                placed = max_st[:].rearrange("p t (g c) -> p t g c", g=G)
                chain(nc.vector.tensor_copy(placed[:, :, :, 0:HG], heads))
                nc.vector.tensor_tensor(placed[:, :, :, HG:2 * HG], heads, placed[:, :, :, 0:HG].bitcast(F32),
                                        ALU.subtract).then_inc(max_st_ready, 1)

            def store(n):
                if n >= 2:
                    dve.wait_ge(out_done[n % 2], 16 * (n // 2))
                for k, tok in enumerate(shares((n + 1) * NU - 1)):
                    dve.wait_ge(down_done, (n + 1) * NU + k)
                    nc.vector.tensor_tensor(y_sb[:, n % 2].rearrange("p t d -> p (t d)")[:, tok],
                                            acc_of(n, tok.start // P)[:, tok],
                                            x2[:, n].rearrange("p t d -> p (t d)")[:, tok], ALU.add)\
                        .then_inc(y_ready, 1)

            dve.wait_ge(ld_x[0], 16)
            moments(0, 0, x_sb)
            dve.wait_ge(ld["wq"], 16)
            chain(nc.vector.tensor_copy(wq_hi[:], wq_sb[:]))
            nc.vector.tensor_tensor(wq_lo[:], wq_sb[:], wq_hi[:].bitcast(F32), ALU.subtract).then_inc(wq_split, 1)
            dve.wait_ge(zeroed, 3)
            for kind, b, g in PLAN:
                if kind == "k":
                    a = slice(QUAD * quads(b)[2], QUAD * quads(b)[2] + QUAD)
                    dve.wait_ge(k_hi_ready, b + 1)
                    nc.vector.tensor_tensor(k_st[a, b], bank("k", b, 0)[a, 0:B * SK], k_st[a, b].bitcast(F32),
                                            ALU.subtract).then_inc(k_st_ready, 1)
                elif kind == "v":
                    if b == 0:
                        dve.wait_ge(ld["v_mask"], 16)
                    dve.wait_ge(*filled_by("v", b, 0))
                    for j, (a, z) in enumerate(KC):
                        ins = nc.vector.tensor_tensor(v_bd[0:z - a, b, j], v_mask[0:z - a, j],
                                                      bank("v", b, 0)[0:z - a, j * D:(j + 1) * D], ALU.mult)
                    ins.then_inc(v_bd_ready, 1)
                elif kind == "moments":
                    dve.wait_ge(ld_x[b], 16)
                    moments(0, b, x_sb)
                elif kind == "norm":
                    normalise(0, b, x_sb)
                elif kind == "xt":
                    low_part(xt_lo[:], xt_hi[:], "xt", b, 0, hi_ready=xt_hi_ready, done=xt_lo_ready)
                elif kind == "q":
                    dve.wait_ge(q_hi_ready, b + 1)
                    nc.vector.scalar_tensor_tensor(
                        out=q_lo[:], in0=bank("q", b, g)[:, 0:S], scalar=bq_sb[:], in1=q_hi[:].bitcast(F32),
                        op0=ALU.add, op1=ALU.subtract).then_inc(q_lo_ready, 1)
                elif kind == "sq":
                    row_maximum(b, g)
                elif kind == "place_max":
                    place_maximum(b)
                elif kind == "den":
                    dve.wait_ge(*filled_by("den", b, 0))
                    nc.vector.reciprocal(den_inv[:].rearrange("p t h -> p (t h)"),
                                         bank("den", b, 0)[:].rearrange("p (n d) -> p n d", d=HD)[:, :, 0])\
                        .then_inc(den_inv_ready, 1)
                    dve.wait_ge(den_inv_ready, b + 1)
                    nc.vector.tensor_copy(den_rep[:].rearrange("p t (h d) -> p (t h) d", d=HD),
                                          den_inv[:].rearrange("p t h -> p (t h)").unsqueeze(2)
                                          .to_broadcast([P, T * H, HD])).then_inc(den_rep_ready, 1)
                elif kind == "inv":
                    dve.wait_ge(inv_t_ready, b + 1)
                    nc.vector.tensor_tensor(att_t[:], po[:], inv_t[:], ALU.mult).then_inc(att_ready, 1)
                elif kind == "wo":
                    dve.wait_ge(*filled_by("wo", b, 0))
                    dve.wait_ge(x_bo_ready, b + 1)
                    nc.vector.tensor_tensor(x2[:, b].rearrange("p t d -> p (t d)"), bank("wo", b, 0)[:],
                                            x2[:, b].rearrange("p t d -> p (t d)"), ALU.add)\
                        .then_inc(x2_ready, 1)
                    dve.wait_ge(x2_ready, b + 1)
                    moments(1, b, x2)
                elif kind == "midnorm":
                    normalise(1, b, x2)
                elif kind == "x2t":
                    low_part(x2t_lo[:, b * S:(b + 1) * S], x2t_hi[:, b * S:(b + 1) * S], "x2t", b, 0,
                             hi_ready=x2t_hi_ready, done=x2t_lo_ready)
                elif kind == "split_router":
                    dve.wait_ge(ld["rw"], 16)
                    chain(nc.vector.tensor_copy(rw_st[:, 0], rw_sb[:]))
                    nc.vector.tensor_tensor(rw_st[:, 1], rw_sb[:], rw_st[:, 0].bitcast(F32), ALU.subtract)\
                        .then_inc(rw_split, 1)
                elif kind == "route":
                    route(b)
                elif kind == "combine":
                    combine_weights(b)
                elif kind == "unit":
                    expert(b, g)
                elif kind == "store":
                    store(b)

        @block.tensor
        def _(pe):
            def take(*use):
                if before[use]:
                    pe.wait_ge(*released(*before[use]))
                return banks[bank_of[use]], bank_ready[bank_of[use]]

            def transposes(src, *use):
                ps, ready = take(*use)
                for t in range(T):
                    ins = nc.tensor.transpose(ps[:, t * P:(t + 1) * P], src(t), ident)
                ins.then_inc(ready, 1)

            def gate_up(n, p):
                tok = slice(n * S, (n + 1) * S)
                if p == 0:
                    pe.wait_ge(x2t_hi_ready, n + 1)
                    pe.wait_ge(x2t_lo_ready, n + 1)
                for kind, hi, lo in (("gate", wg_hi, wg_lo), ("up", wu_hi, wu_lo)):
                    ps, ready = take(kind, n, p)
                    nc.tensor.matmul(ps[:], hi[:, p], x2t_hi[:, tok], start=True, stop=False)
                    nc.tensor.matmul(ps[:], hi[:, p], x2t_lo[:, tok], start=False, stop=False)
                    nc.tensor.matmul(ps[:], lo[:, p], x2t_hi[:, tok], start=False, stop=True).then_inc(ready, 1)
                if p > 0:
                    ps, ready = take("spread", n, p)
                    if p == 1:
                        pe.wait_ge(comb_t_ready, n + 1)
                    nc.tensor.matmul(ps[:], sel[:, 2 * p - 2:2 * p].rearrange("p e f -> p (e f)"),
                                     comb_t[:, tok], start=True, stop=True).then_inc(ready, 1)

            def down_proj(n, p):
                u = n * NU + p
                if p == 0:
                    pe.wait_ge(den_copied, weighed_before[n])
                    if n > 0:
                        pe.wait_ge(y_ready, n)
                    if n == B - 1:
                        pe.wait_ge(att_ready, B)
                for k, tok in enumerate(shares(u)):
                    pe.wait_ge(hid_ready, u + 1 + k)
                    for t in range(tok.start // P, tok.stop // P):
                        first = t == 0 or acc_of(n, t) is not acc_of(n, t - 1)
                        ins = nc.tensor.matmul(acc_of(n, t)[:, t * D:(t + 1) * D], hid[:, u % 3, t * P:(t + 1) * P],
                                               wd_sb[:, p], start=(p == 0 and first), stop=(p == NU - 1),
                                               skip_group_check=True)
                    ins.then_inc(down_done, 1)

            pe.wait_ge(ld["ctx"], 16)
            pe.wait_ge(ld["wk"], 16)
            for kind, b, g in PLAN:
                if kind == "k":
                    ps, ready = take("k", b, 0)
                    nc.tensor.matmul(ps[:, 0:B * SK], wk_sb[:, b], ctx_sb[:].rearrange("c b k -> c (b k)"),
                                     start=True, stop=True).then_inc(ready, 1)
                elif kind == "xt":
                    if b == 0:
                        pe.wait_ge(ld["consts"], 16)
                    pe.wait_ge(xn_ready[0], b + 1)
                    transposes(lambda t: xn[:, 0, t], "xt", b, 0)
                elif kind == "v":
                    ps, ready = take("v", b, 0)
                    pe.wait_ge(ctx_rep_ready, b + 1)
                    if b == 0:
                        pe.wait_ge(ld["wv"], 16)
                    for j, (a, z) in enumerate(KC):
                        ins = nc.tensor.matmul(ps[0:z - a, j * D:(j + 1) * D],
                                               ctx_rep[:, b].rearrange("c h k -> c (h k)")[:, a:z], wv_sb[:],
                                               start=True, stop=True)
                    ins.then_inc(ready, 1)
                elif kind == "q":
                    ps, ready = take("q", b, g)
                    if b == 0 and g == 0:
                        pe.wait_ge(wq_split, 1)
                    pe.wait_ge(xt_hi_ready, b + 1)
                    nc.tensor.matmul(ps[:, 0:S], wq_hi[:], xt_hi[:], start=True, stop=False)
                    nc.tensor.matmul(ps[:, 0:S], wq_lo[:], xt_hi[:], start=False, stop=False)
                    pe.wait_ge(xt_lo_ready, b + 1)
                    nc.tensor.matmul(ps[:, 0:S], wq_hi[:], xt_lo[:], start=False, stop=True).then_inc(ready, 1)
                elif kind == "place_q":
                    ps, ready = take("place_q", b, g)
                    if b == 0:
                        pe.wait_ge(place_ready, g + 1)
                    if g == 0:
                        pe.wait_ge(q_hi_ready, b + 1)
                    nc.tensor.matmul(ps[:, 0:S], place[:, 0, g], q_hi[:], start=True, stop=False)
                    if g == 0:
                        pe.wait_ge(q_lo_ready, b + 1)
                    nc.tensor.matmul(ps[:, 0:S], place[:, 1, g], q_lo[:], start=False, stop=True).then_inc(ready, 1)
                elif kind == "sq":
                    t, gr = g // G, g % G
                    ps, ready = take("sq", b, g)
                    if t == 0:
                        pe.wait_ge(q_st_ready, b * G + gr + 1)
                        pe.wait_ge(k_bd_ready, b * G + gr + 1)
                    nc.tensor.matmul(ps[:, 0:GK], q_st[:, b % 2, gr, t * P:(t + 1) * P], k_bd[:, gr, b],
                                     start=True, stop=True).then_inc(ready, 1)
                elif kind == "max":
                    pe.wait_ge(max_st_ready, b + 1)
                    transposes(lambda t: max_st[:, t].bitcast(F32), "max", b, 0)
                elif kind == "st":
                    j, gr = g // G, g % G
                    a, z = KC[j]
                    ps, ready = take("st", b, g)
                    if j == 0:
                        pe.wait_ge(q_max_ready, b * G + gr + 1)
                    nc.tensor.matmul(ps[0:z - a, :], k_bd[:, gr, b, a:z], q_st[:, b % 2, gr],
                                     start=True, stop=True).then_inc(ready, 1)
                elif kind == "weigh":
                    a, z = KC[g]
                    if g == 0:
                        pe.wait_ge(v_bd_ready, b + 1)
                        if b > 0:
                            pe.wait_ge(den_copied, b)
                            pe.wait_ge(att_ready, b)
                        if stored_before[b]:
                            pe.wait_ge(y_ready, stored_before[b])
                    for out_ps, lhs in ((po, v_bd[0:z - a, b, g]), (pd, v_mask[0:z - a, g])):
                        for gr in range(G):
                            e = b * NJ * G + g * G + gr
                            pe.wait_ge(exp_done, e + 1)
                            q = slice(QUAD * gr, QUAD * (gr + 1))
                            ins = nc.tensor.matmul(out_ps[q, :], lhs[:, q], probs[0:z - a, e % 8],
                                                   start=(g == 0), stop=(g == NJ - 1))
                    ins.then_inc(pv_done, 1)
                elif kind == "den":
                    pe.wait_ge(den_copied, b + 1)
                    transposes(lambda t: den_sb[:, t * P:(t + 1) * P], "den", b, 0)
                elif kind == "inv":
                    pe.wait_ge(den_rep_ready, b + 1)
                    transposes(lambda t: den_rep[:, t], "inv", b, 0)
                elif kind == "wo":
                    ps, ready = take("wo", b, 0)
                    if b == 0:
                        pe.wait_ge(ld["wo"], 16)
                    pe.wait_ge(att_ready, b + 1)
                    for t in range(T):
                        ins = nc.tensor.matmul(ps[:, t * D:(t + 1) * D], att_t[:, t * P:(t + 1) * P], wo_sb[:],
                                               start=True, stop=True)
                    ins.then_inc(ready, 1)
                elif kind == "x2t":
                    pe.wait_ge(xn_ready[1], b + 1)
                    transposes(lambda t: xn[:, 1, t], "x2t", b, 0)
                elif kind == "router":
                    ps, ready = take("router", b, 0)
                    if b == 0:
                        pe.wait_ge(rw_split, 1)
                    pe.wait_ge(x2t_hi_ready, b + 1)
                    pe.wait_ge(x2t_lo_ready, b + 1)
                    for t in range(T):
                        tok = slice(b * S + t * P, b * S + (t + 1) * P)
                        nc.tensor.matmul(ps[:, t * 2 * E:t * 2 * E + E], x2t_lo[:, tok], rw_st[:, 0],
                                         start=True, stop=False, skip_group_check=True)
                        ins = nc.tensor.matmul(ps[:, t * 2 * E:(t + 1) * 2 * E], x2t_hi[:, tok],
                                               rw_st[:].rearrange("p a e -> p (a e)"), start=False, stop=True,
                                               skip_group_check=True)
                    ins.then_inc(ready, 1)
                elif kind == "comb":
                    pe.wait_ge(comb_st_ready, b + 1)
                    transposes(lambda t: comb_st[:, t].bitcast(F32), "comb", b, 0)
                elif kind == "unit":
                    if b == 0 and g == 0:
                        pe.wait_ge(w_lo_ready, 2)
                        pe.wait_ge(sel_ready, 1)
                        pe.wait_ge(ld["wd"], 32)
                    gate_up(b, g)
                elif kind == "down":
                    down_proj(b, g)


_ARGS = ["x", "ctx_t", "wq", "bq", "wk", "wv", "wo", "bo", "router_t", "router_bias", "up", "gate", "down",
         "sh_gate_t", "sh_up_t", "sh_down_t", "consts", "v_mask"]


def kernel(**inputs):
    import numpy as np
    from concourse import bacc
    from concourse.bass_utils import run_bass_kernel_spmd

    a = {n.replace("L0_xattn_", "").replace("L0_ffn_", ""): np.asarray(v) for n, v in inputs.items()}
    x, y = a["x"], a["ctx_768"]
    B, SK, C = y.shape
    D = x.shape[2]
    E = a["up_proj"].shape[0]
    QUAD, G, HG, P = 32, 4, 4, 128
    HD = D // (G * HG)
    chunks = [(0, 104), (104, 206), (206, 308)]

    ctx_t = np.ones((C + 1, B, SK), x.dtype)
    ctx_t[:C] = y.transpose(2, 0, 1)
    wk = np.zeros((C + 1, G, P), x.dtype)
    for g in range(G):
        cols = slice(QUAD * g, QUAD * (g + 1))
        for a4 in range(4):
            here = slice(QUAD * a4, QUAD * (a4 + 1))
            if a4 != g:
                wk[:C, g, here] = a["wk"][:, cols]
                wk[C, g, here] = a["bk"][cols]
            else:
                wk[C, g, here] = 1.0
    wv = np.concatenate([a["wv"], a["bv"][None]], 0)

    row = np.arange(P)
    k_mask = np.zeros((P, G, HG), x.dtype)
    for g in range(G):
        for h in range(HG):
            k_mask[:, g, h] = (row % QUAD) // HD == h
            own = row // QUAD == g
            k_mask[own, g, h] = ((row % QUAD) % HG == h)[own] & ((row % QUAD) < 2 * HG)[own]
    v_mask = np.zeros((P, len(chunks), D), x.dtype)
    for j, (lo, hi) in enumerate(chunks):
        for r in range(hi - lo):
            v_mask[r, j] = (np.arange(D) % QUAD) // HD == (lo + r) // SK
    pair_rows = np.zeros((P, E), x.dtype)
    for e in range(E):
        pair_rows[e, e] = pair_rows[QUAD + e, e] = 1.0
    iota = np.tile(np.arange(E, dtype=x.dtype), (P, 1))
    consts = np.concatenate([np.eye(P, dtype=x.dtype), k_mask.reshape(P, -1), pair_rows, iota], 1)

    laid = {
        "x": x, "ctx_t": ctx_t, "wq": a["wq"], "bq": a["bq"].reshape(D, 1), "wk": wk, "wv": wv,
        "wo": a["wo"], "bo": a["bo"],
        "router_t": a["router_w"].T, "router_bias": a["router_bias"], "up": a["up_proj"], "gate": a["gate_proj"],
        "down": a["down_proj"], "sh_gate_t": a["sh_gate"].T, "sh_up_t": a["sh_up"].T, "sh_down_t": a["sh_down"].T,
        "consts": consts, "v_mask": v_mask,
    }
    nc = bacc.Bacc("TRN2", target_bir_lowering=False, num_devices=1)
    arrays, aps = {}, []
    for name in _ARGS:
        arr = np.ascontiguousarray(laid[name])
        arrays[f"in_{name}"] = arr
        aps.append(nc.dram_tensor(f"in_{name}", arr.shape, mybir.dt.from_np(arr.dtype), kind="ExternalInput").ap())
    aps.append(nc.dram_tensor("out_y", x.shape, F32, kind="ExternalOutput").ap())
    build(nc, *aps)
    r = run_bass_kernel_spmd(nc, [arrays], core_ids=[0])
    return r.results[0]["out_y"]
```
